# Optimizing a Trainium2 kernel written in Bass

```python
import numpy as np
import jax
import jax.numpy as jnp

def _softmax(x, axis=-1):
    return jax.nn.softmax(x, axis=axis)

def _gelu(x):
    return jax.nn.gelu(x, approximate=True)

def _silu(x):
    return jax.nn.silu(x)

def _sigmoid(x):
    return jax.nn.sigmoid(x)

def _layernorm(x, axis=-1, eps=1e-05):
    m = jnp.mean(x, axis=axis, keepdims=True)
    v = jnp.var(x, axis=axis, keepdims=True)
    return (x - m) / jnp.sqrt(v + eps)

def _scatter_add(tgt, idx, src, axis=0):
    return tgt.at[idx].add(src)

def _segment_sum(src, seg, n):
    return jax.ops.segment_sum(src, seg, n)
kernel_name = 'mk_recurrent_d1_jaxref_r8_84aeb4'

def setup_inputs(seed: int=0):
    np.random.seed(seed)
    _w = jnp.asarray

    def _L0_attn_setup():
        import jax, jax.numpy as jnp
        import numpy as np
        H = 512
        D = 1024
        N = 16
        K = 4
        R = 32
        BATCH = 1
        L = 256
        EPS = 1e-06

        def _rmsnorm(x, w):
            return x * jax.lax.rsqrt(jnp.mean(x * x, axis=-1, keepdims=True) + EPS) * w
        key = jax.random.key(seed)
        ks = jax.random.split(key, 10)
        s = 0.02
        return {'hidden_states': jax.random.normal(ks[0], (BATCH, L, H), jnp.float32), 'W_in': jax.random.normal(ks[1], (2 * D, H), jnp.float32) * s, 'conv_w': jax.random.normal(ks[2], (D, K), jnp.float32) * s, 'conv_b': jax.random.normal(ks[3], (D,), jnp.float32) * s, 'Wx': jax.random.normal(ks[4], (R + 2 * N, D), jnp.float32) * s, 'dt_ln_w': jnp.ones((R,), jnp.float32), 'b_ln_w': jnp.ones((N,), jnp.float32), 'c_ln_w': jnp.ones((N,), jnp.float32), 'Wdt': jax.random.normal(ks[5], (D, R), jnp.float32) * s, 'dt_bias': jax.random.normal(ks[6], (D,), jnp.float32) * s, 'A': -jnp.exp(jax.random.normal(ks[7], (D, N), jnp.float32) * 0.5), 'D_param': jnp.ones((D,), jnp.float32), 'W_out': jax.random.normal(ks[8], (H, D), jnp.float32) * s}
    _L0_attn_in = _L0_attn_setup()

    def _L0_ffn_setup():
        import jax, jax.numpy as jnp
        import numpy as np
        HIDDEN = 512
        INTER = 1376
        key = jax.random.key(seed)
        k0, k1, k2, k3 = jax.random.split(key, 4)
        scale_h = 1.0 / np.sqrt(HIDDEN)
        scale_i = 1.0 / np.sqrt(INTER)
        return {'x': jax.random.normal(k0, (4, 32, HIDDEN), dtype=jnp.float32), 'w_gate': jax.random.normal(k1, (INTER, HIDDEN), dtype=jnp.float32) * scale_h, 'w_up': jax.random.normal(k2, (INTER, HIDDEN), dtype=jnp.float32) * scale_h, 'w_down': jax.random.normal(k3, (HIDDEN, INTER), dtype=jnp.float32) * scale_i}
    _L0_ffn_in = _L0_ffn_setup()
    _d = {'L0_attn_hidden_states': _L0_attn_in['hidden_states'], 'L0_attn_W_in': _L0_attn_in['W_in'], 'L0_attn_conv_w': _L0_attn_in['conv_w'], 'L0_attn_conv_b': _L0_attn_in['conv_b'], 'L0_attn_Wx': _L0_attn_in['Wx'], 'L0_attn_dt_ln_w': _L0_attn_in['dt_ln_w'], 'L0_attn_b_ln_w': _L0_attn_in['b_ln_w'], 'L0_attn_c_ln_w': _L0_attn_in['c_ln_w'], 'L0_attn_Wdt': _L0_attn_in['Wdt'], 'L0_attn_dt_bias': _L0_attn_in['dt_bias'], 'L0_attn_A': _L0_attn_in['A'], 'L0_attn_D_param': _L0_attn_in['D_param'], 'L0_attn_W_out': _L0_attn_in['W_out'], 'L0_ffn_w_gate': _L0_ffn_in['w_gate'], 'L0_ffn_w_up': _L0_ffn_in['w_up'], 'L0_ffn_w_down': _L0_ffn_in['w_down']}
    _x0 = _d['L0_attn_hidden_states']
    _d['L0_attn_hidden_states'] = jax.random.normal(jax.random.fold_in(jax.random.key(seed), 1), (4, 512, 512), dtype=_x0.dtype)
    del _x0
    return _d

def reference(L0_attn_hidden_states, L0_attn_W_in, L0_attn_conv_w, L0_attn_conv_b, L0_attn_Wx, L0_attn_dt_ln_w, L0_attn_b_ln_w, L0_attn_c_ln_w, L0_attn_Wdt, L0_attn_dt_bias, L0_attn_A, L0_attn_D_param, L0_attn_W_out, L0_ffn_w_gate, L0_ffn_w_up, L0_ffn_w_down):

    def _L0_attn_ref(hidden_states, W_in, conv_w, conv_b, Wx, dt_ln_w, b_ln_w, c_ln_w, Wdt, dt_bias, A, D_param, W_out):
        import jax, jax.numpy as jnp
        import numpy as np
        H = 512
        D = 1024
        N = 16
        K = 4
        R = 32
        BATCH = 1
        L = 256
        EPS = 1e-06

        def _rmsnorm(x, w):
            return x * jax.lax.rsqrt(jnp.mean(x * x, axis=-1, keepdims=True) + EPS) * w
        proj = hidden_states @ W_in.T
        u, gate = jnp.split(proj, 2, axis=-1)
        x = jnp.transpose(u, (0, 2, 1))
        x = jax.lax.conv_general_dilated(x, conv_w[:, None, :], window_strides=(1,), padding=[(K - 1, 0)], dimension_numbers=('NCH', 'OIH', 'NCH'), feature_group_count=D)
        u = jax.nn.silu(jnp.transpose(x, (0, 2, 1)) + conv_b)
        ssm_p = u @ Wx.T
        dt, Bm, Cm = jnp.split(ssm_p, [R, R + N], axis=-1)
        dt = _rmsnorm(dt, dt_ln_w)
        Bm = _rmsnorm(Bm, b_ln_w)
        Cm = _rmsnorm(Cm, c_ln_w)
        delta = jax.nn.softplus(dt @ Wdt.T + dt_bias)

        def step(state, xs):
            d_t, B_t, C_t, u_t = xs
            dA = jnp.exp(d_t[..., None] * A)
            state = dA * state + (d_t * u_t)[..., None] * B_t[:, None, :]
            y_t = jnp.einsum('bdn,bn->bd', state, C_t)
            return (state, y_t)
        init = jnp.zeros((hidden_states.shape[0], D, N), hidden_states.dtype)
        xs = (jnp.swapaxes(delta, 0, 1), jnp.swapaxes(Bm, 0, 1), jnp.swapaxes(Cm, 0, 1), jnp.swapaxes(u, 0, 1))
        _, ys = jax.lax.scan(step, init, xs)
        y = jnp.swapaxes(ys, 0, 1) + u * D_param
        y = y * jax.nn.silu(gate)
        return y @ W_out.T

    def _L0_ffn_ref(x, w_gate, w_up, w_down):
        import jax, jax.numpy as jnp
        import numpy as np
        HIDDEN = 512
        INTER = 1376
        gate = jax.nn.silu(jnp.einsum('bsh,ih->bsi', x, w_gate))
        up = jnp.einsum('bsh,ih->bsi', x, w_up)
        return jnp.einsum('bsi,hi->bsh', gate * up, w_down)
    x = L0_attn_hidden_states
    xn = _layernorm(x, axis=-1)
    s = _L0_attn_ref(xn, L0_attn_W_in, L0_attn_conv_w, L0_attn_conv_b, L0_attn_Wx, L0_attn_dt_ln_w, L0_attn_b_ln_w, L0_attn_c_ln_w, L0_attn_Wdt, L0_attn_dt_bias, L0_attn_A, L0_attn_D_param, L0_attn_W_out)
    g = _silu(_L0_ffn_ref(xn, L0_ffn_w_gate, L0_ffn_w_up, L0_ffn_w_down))
    x = x + s * g
    return x

_drawn_inputs = setup_inputs


def setup_inputs(seed=0):
    import zlib

    import numpy as np

    out = dict(_drawn_inputs(seed))
    spreads = {'L0_attn_dt_ln_w': (1.0, 0.2),
     'L0_attn_b_ln_w': (1.0, 0.2),
     'L0_attn_c_ln_w': (1.0, 0.2),
     'L0_attn_D_param': (1.0, 0.2)}
    factors = {}
    for name, (base, spread) in spreads.items():
        noise = np.random.default_rng([zlib.crc32(name.encode()), seed]).standard_normal(out[name].shape)
        drawn = base * np.exp(spread * noise) if base else spread * noise
        out[name] = jnp.asarray(drawn.astype(out[name].dtype))
    for name, factor in factors.items():
        out[name] = (out[name] * factor).astype(out[name].dtype)
    return out
```

```python
import numpy as np
import concourse.bass as bass
from concourse import mybir
from concourse.alu_op_type import AluOpType as ALU
from contextlib import ExitStack

NB, T, H, D, N, R, KC, I = 4, 512, 512, 1024, 16, 32, 4, 1376
P = 128
KH, KD, KI, TC = H // P, D // P, -(-I // P), T // P
HF = 2
JH = KD // HF
JQ = 2
QH = JH // JQ
UNITS = N * HF
F = R + 2 * N
LN_EPS, RMS_EPS = 1e-5, 1e-6
WD_RING, B_RING, S_RING = 3, 4, 3


def build(nc, x, w_in, w_out, w_x, w_dt, conv_w, conv_b, dt_b, a_par, d_par, ln_w, w_gu, w_dn, ident_d, out):
    fp32 = mybir.dt.float32
    ACT = mybir.ActivationFunctionType
    AX = mybir.AxisListType
    ctx = ExitStack()
    with ctx:
        def sb(name, shape):
            return ctx.enter_context(nc.sbuf_tensor("sb_" + name, shape, fp32))

        def sem(name):
            return ctx.enter_context(nc.semaphore(name))

        wout = sb("wout", [P, KD, H])
        wx = sb("wx", [P, KD, F])
        wdt = sb("wdt", [R, D])
        cw = sb("cw", [P, KD, KC])
        cb = sb("cb", [P, KD])
        dtb = sb("dtb", [P, KD])
        apar = sb("apar", [P, KD, N])
        dpar = sb("dpar", [P, KD])
        lnw = sb("lnw", [P, F])
        ident = sb("ident", [P, P])
        half = sb("half", [P, 3 * TC])
        win = sb("win", [P, KH, D])
        wgu = sb("wgu", [P, 2, 2, KH, P])
        wdn = sb("wdn", [P, WD_RING, H])
        xnT = sb("xnT", [P, KH, T])
        u = sb("u", [P, KD, T])
        delta = sb("delta", [P, KD, T])
        v = sb("v", [P, KD, T])
        nrm = sb("nrm", [P, TC, F])
        dtB = sb("dtB", [R + N, T])
        bb = sb("bb", [P, B_RING, T])
        dA = sb("dA", [P, S_RING, JQ, T])
        dBu = sb("dBu", [P, S_RING, JQ, T])
        h = sb("h", [P, 2, JH, T])
        yT = sb("yT", [P, TC, D])
        gffn = sb("gffn", [P, TC, H])
        S = sb("S", [P, KI, T])
        stats = sb("stats", [P, TC, 6])
        mv = sb("mv", [P, 3, TC])
        rstd = sb("rstd", [P, 2, TC])
        ms = sb("ms", [P, 3, TC, 3])
        xt = S[:, 0:TC, :]
        acc_r = [S[:, 4 + r, :] for r in range(2)]
        tmp_r = [S[:, 6 + r, :] for r in range(2)]
        ssm = S[:, 10, 0:TC * F].rearrange("p (c f) -> p c f", f=F)
        sg_r = [S[:, r, :] for r in range(2)]
        xres = S[:, 4:4 + TC, :]
        o_r = [S[:, 8 + r, :] for r in range(2)]

        pj = [ctx.enter_context(nc.psum_tensor(f"pj{i}", [P, T], fp32)) for i in range(4)]
        hT = [ctx.enter_context(nc.psum_tensor(f"hT{i}", [P, T], fp32)) for i in range(TC)]
        b_dram = nc.dram_tensor("b_rows", [N, T], fp32, kind="Internal").ap()

        const_in = sem("const_in")
        init_done = sem("init_done")
        half_done = sem("half_done")
        x_in = sem("x_in")
        win_in = sem("win_in")
        ln_stat = sem("ln_stat")
        ln_aggr = sem("ln_aggr")
        ln_var = sem("ln_var")
        ln_rstd = sem("ln_rstd")
        xn_done = sem("xn_done")
        xT_ps = sem("xT_ps")
        xT_done = sem("xT_done")
        u_ps = sem("u_ps")
        tap0_done = sem("tap0_done")
        tap_done = sem("tap_done")
        th_done = sem("th_done")
        u_done = sem("u_done")
        ssm_ps = sem("ssm_ps")
        sq_done = sem("sq_done")
        ms_done = sem("ms_done")
        mse_done = sem("mse_done")
        rms_done = sem("rms_done")
        nm_done = sem("nm_done")
        nrm_done = sem("nrm_done")
        dtT_ps = sem("dtT_ps")
        dtT_done = sem("dtT_done")
        b_out = sem("b_out")
        b_in = [sem(f"b_in{r}") for r in range(B_RING)]
        z_ps = sem("z_ps")
        sp_done = sem("sp_done")
        lin_done = sem("lin_done")
        del_done = sem("del_done")
        v_done = sem("v_done")
        dA_done = sem("dA_done")
        dBu_done = sem("dBu_done")
        scan_done = sem("scan_done")
        hT_ps = sem("hT_ps")
        y_done = sem("y_done")
        wgu_in = [sem(f"wgu_in{r}") for r in range(2)]
        wdn_in = [sem(f"wdn_in{r}") for r in range(WD_RING)]
        fg_ps = sem("fg_ps")
        fu_ps = sem("fu_ps")
        fth_done = sem("fth_done")
        fs_done = sem("fs_done")
        f_done = sem("f_done")
        dn_used = sem("dn_used")
        gth_done = sem("gth_done")
        g_done = sem("g_done")
        gt_ps = sem("gt_ps")
        yb_ps = sem("yb_ps")
        gtt_done = sem("gtt_done")
        sg_done = sem("sg_done")
        yu_done = sem("yu_done")
        yg_done = sem("yg_done")
        o_ps = sem("o_ps")
        og_done = sem("og_done")
        o_done = sem("o_done")
        xr_in = sem("xr_in")
        out_dma = [sem(f"out_dma{r}") for r in range(2)]

        consts = [(wout, w_out), (wx, w_x), (wdt, w_dt), (cw, conv_w), (cb, conv_b), (dtb, dt_b),
                  (apar, a_par), (dpar, d_par), (ident, ident_d)]
        N_CONST = 16 * (len(consts) + 1)

        def ffn_slots(i):
            first_down = 2 * KI
            if i < first_down:
                return i // 2, i % 2, []
            share = [first_down + (t * (UNITS - first_down)) // KI for t in range(KI)]
            return None, None, [t for t in range(KI) if share[t] == i]

        block = ctx.enter_context(nc.Block())

        @block.sync
        def _(sp):
            for dst, src in consts:
                sp.dma_start(dst[:], src).then_inc(const_in, 16)
            sp.dma_start(lnw[:, :], ln_w.partition_broadcast(P)).then_inc(const_in, 16)
            with sp.Fori(0, NB) as b:
                sp.wait_ge(yg_done, 1 + b * KD)
                sp.dma_start(xt, x[bass.ds(b, 1), :, :].rearrange("o (c p) h -> p (o c) h", p=P)).then_inc(x_in, 16)
                sp.dma_start(win[:, :, :], w_in[0]).then_inc(win_in, 16)
                for t in range(2):
                    sp.dma_start(wgu[:, t % 2], w_gu[t]).then_inc(wgu_in[t % 2], 16)
                for t in range(WD_RING):
                    sp.dma_start(wdn[:, t, :], w_dn[t]).then_inc(wdn_in[t], 16)
                sp.wait_ge(dtT_done, b + 1)
                sp.dma_start(b_dram, dtB[R:R + N, :]).then_inc(b_out, 16)
                sp.wait_ge(b_out, (b + 1) * 16)
                for n in range(B_RING):
                    sp.dma_start(bb[:, n, :], b_dram[n, :].partition_broadcast(P)).then_inc(b_in[n], 16)
                sp.wait_ge(u_ps, (b + 1) * KD)
                sp.dma_start(win[:, :, :], w_in[1]).then_inc(win_in, 16)
                for n in range(N):
                    if n + B_RING < N:
                        sp.wait_ge(dBu_done, b * UNITS * QH + (n + 1) * HF * QH)
                        m = n + B_RING
                        sp.dma_start(bb[:, m % B_RING, :], b_dram[m, :].partition_broadcast(P)).then_inc(b_in[m % B_RING], 16)
                    if n + 2 < KI:
                        sp.wait_ge(fu_ps, b * KI + n + 1)
                        sp.dma_start(wgu[:, n % 2], w_gu[n + 2]).then_inc(wgu_in[n % 2], 16)
                for t in range(WD_RING, KI):
                    sp.wait_ge(dn_used, b * KI + t - WD_RING + 1)
                    sp.dma_start(wdn[:, t % WD_RING, :], w_dn[t]).then_inc(wdn_in[t % WD_RING], 16)
                sp.wait_ge(dn_used, (b + 1) * KI)
                sp.dma_start(xres, x[bass.ds(b, 1), :, :].rearrange("o (c p) h -> p (o c) h", p=P)).then_inc(xr_in, 16)

        @block.scalar
        def _(act):
            act.wait_ge(const_in, N_CONST)
            act.wait_ge(init_done, 3)
            act.wait_ge(half_done, 2)
            with act.Fori(0, NB) as b:
                for k in range(KH):
                    act.wait_ge(xT_ps, b * KH + k + 1)
                    nc.scalar.copy(xnT[:, k, :], pj[k][:, :]).then_inc(xT_done, 1)
                for j in range(KD + 1):
                    if j < KD:
                        act.wait_ge(u_ps, b * KD + j + 1)
                        if j >= 2:
                            act.wait_ge(u_done, b * KD + j - 1)
                        nc.scalar.activation(acc_r[j % 2], pj[j % 4][:, :], ACT.Identity, bias=cb[:, j:j + 1],
                                             scale=cw[:, j, KC - 1:KC]).then_inc(tap0_done, 1)
                    if j > 0:
                        i = j - 1
                        act.wait_ge(tap_done, (b * KD + i + 1) * (KC - 1))
                        nc.scalar.activation(tmp_r[i % 2], acc_r[i % 2], ACT.Tanh).then_inc(th_done, 1)
                act.wait_ge(ssm_ps, b + 1)
                p_ssm = pj[0][:, 0:TC * F].rearrange("p (c f) -> p c f", f=F)
                nc.scalar.activation(nrm[:, :, :], p_ssm, ACT.Square).then_inc(sq_done, 1)
                nc.scalar.copy(ssm[:, :, :], p_ssm).then_inc(sq_done, 1)
                act.wait_ge(dtT_ps, b + 1)
                nc.scalar.copy(dtB[:, :], pj[1][0:R + N, :]).then_inc(dtT_done, 1)
                nc.scalar.preload_act_table_set("natural_log_exp_and_others")
                for j in range(KD):
                    act.wait_ge(z_ps, b * KD + j + 1)
                    if j >= 2:
                        act.wait_ge(del_done, b * KD + j - 1)
                    a = acc_r[j % 2]
                    k = b * 3 * KD + 3 * j
                    nc.scalar.activation(a, pj[j % 4][:, :], ACT.Abs, bias=dtb[:, j:j + 1]).then_inc(sp_done, 1)
                    act.wait_ge(sp_done, k + 1)
                    nc.scalar.activation(a, a, ACT.Exp, scale=-1.0).then_inc(sp_done, 1)
                    act.wait_ge(sp_done, k + 2)
                    nc.scalar.activation(a, a, ACT.Ln, bias=1.0).then_inc(sp_done, 1)

                for i in range(UNITS):
                    n, hf = i // HF, i % HF
                    for q in range(QH):
                        s = i * QH + q
                        if i == 0:
                            act.wait_ge(del_done, b * KD + (q + 1) * JQ)
                        elif i == 1:
                            act.wait_ge(del_done, b * KD + JH + (q + 1) * JQ)
                        if s >= S_RING:
                            act.wait_ge(scan_done, b * UNITS * QH + s - S_RING + 1)
                        for e in range(JQ):
                            j = hf * JH + q * JQ + e
                            last = nc.scalar.activation(dA[:, s % S_RING, e, 1:T], delta[:, j, 1:T], ACT.Exp,
                                                        scale=apar[:, j, n:n + 1])
                        last.then_inc(dA_done, 1)
                    if i >= 2 and i % 2 == 0 and (i - 2) // 2 < KI:
                        t = (i - 2) // 2
                        act.wait_ge(fg_ps, b * KI + t + 1)
                        if t >= TC:
                            act.wait_ge(fs_done, b * KI + t - TC + 1)
                        nc.scalar.activation(gffn[:, t % TC, :], pj[2 * t % 4][:, :], ACT.Tanh, scale=0.5).then_inc(fth_done, 1)
                act.wait_ge(dn_used, (b + 1) * KI)
                for c in range(TC):
                    if c == 0:
                        act.wait_ge(fs_done, (b + 1) * KI)
                    nc.scalar.activation(gffn[:, c, :], pj[c][:, :], ACT.Tanh, scale=0.5).then_inc(gth_done, 1)
                for j in range(KD):
                    act.wait_ge(gt_ps, b * KD + j + 1)
                    if j >= 2:
                        act.wait_ge(yg_done, 1 + b * KD + j - 1)
                    nc.scalar.activation(sg_r[j % 2], pj[j % 2][:, :], ACT.Tanh, scale=0.5).then_inc(gtt_done, 1)
                for c in range(TC):
                    act.wait_ge(o_done, b * TC + c + 1)
                    act.dma_start(out[bass.ds(b, 1), c * P:(c + 1) * P, :].rearrange("o p h -> p (o h)"),
                                  o_r[c % 2]).then_inc(out_dma[c % 2], 16)
                for r in range(2):
                    act.wait_ge(out_dma[r], (b + 1) * TC * 8)

        @block.gpsimd
        def _(pool):
            pool.wait_ge(init_done, 3)
            with pool.Fori(0, NB) as b:
                pool.wait_ge(ln_var, b + 1)
                nc.gpsimd.tensor_tensor(rstd[:, 1, :], rstd[:, 0, :], half[:, 0:TC], ALU.pow).then_inc(ln_rstd, 1)
                pool.wait_ge(mse_done, (b + 1) * 2)
                nc.gpsimd.tensor_tensor(ms[:, 2].rearrange("p c g -> p (c g)"), ms[:, 1].rearrange("p c g -> p (c g)"),
                                        half[:, :], ALU.pow).then_inc(rms_done, 1)
                for j in range(KD):
                    pool.wait_ge(sp_done, b * 3 * KD + 3 * (j + 1))
                    pool.wait_ge(lin_done, b * KD + j + 1)
                    nc.gpsimd.tensor_tensor(delta[:, j, :], acc_r[j % 2], tmp_r[j % 2], ALU.add).then_inc(del_done, 1)
                    pool.wait_ge(del_done, b * KD + j + 1)
                    nc.gpsimd.tensor_tensor(v[:, j, :], delta[:, j, :], u[:, j, :], ALU.mult).then_inc(v_done, 1)
                pool.wait_ge(v_done, (b + 1) * KD)
                for i in range(UNITS):
                    n, hf = i // HF, i % HF
                    if hf == 0:
                        pool.wait_ge(b_in[n % B_RING], b * (N // B_RING) * 16 + (n // B_RING + 1) * 16)
                    for q in range(QH):
                        s = i * QH + q
                        j = hf * JH + q * JQ
                        if s >= S_RING:
                            pool.wait_ge(scan_done, b * UNITS * QH + s - S_RING + 1)
                        nc.gpsimd.tensor_tensor(dBu[:, s % S_RING, :, :], v[:, j:j + JQ, :],
                                                bb[:, n % B_RING, :].unsqueeze(1).to_broadcast([P, JQ, T]),
                                                ALU.mult).then_inc(dBu_done, 1)
                for j in range(KD):
                    pool.wait_ge(sg_done, b * KD + j + 1)
                    pool.wait_ge(yu_done, b * KD + j + 1)
                    nc.gpsimd.tensor_tensor(u[:, j, :], u[:, j, :], sg_r[j % 2], ALU.mult).then_inc(yg_done, 1)
                pool.wait_ge(xr_in, (b + 1) * 16)
                for c in range(TC):
                    pool.wait_ge(og_done, 1 + b * TC + c + 1)
                    nc.gpsimd.tensor_tensor(o_r[c % 2], o_r[c % 2], xres[:, c, :], ALU.add).then_inc(o_done, 1)

        @block.vector
        def _(dve):
            nc.vector.memset(half[:, :], -0.5).then_inc(init_done, 1)
            for e in range(JQ):
                nc.vector.memset(dA[:, :, e, 0:1], 0.0).then_inc(init_done, 1)
            nc.vector.memset(mv[:, 0, :], 0.0).then_inc(yg_done, 1)
            nc.vector.memset(mv[:, 1, :], 0.0).then_inc(og_done, 1)
            dve.wait_ge(const_in, N_CONST)
            nc.vector.tensor_scalar(cw[:, :, :], cw[:, :, :], 0.5, None, ALU.mult).then_inc(half_done, 1)
            nc.vector.tensor_scalar(cb[:, :], cb[:, :], 0.5, None, ALU.mult).then_inc(half_done, 1)
            dve.wait_ge(half_done, 2)
            with dve.Fori(0, NB) as b:
                dve.wait_ge(x_in, (b + 1) * 16)
                for c in range(TC):
                    nc.vector.bn_stats(stats[:, c, :], xt[:, c, :]).then_inc(ln_stat, 1)
                dve.wait_ge(ln_stat, (b + 1) * TC)
                nc.vector.tensor_tensor(mv[:, 0, :], stats[:, :, 1], stats[:, :, 4], ALU.add).then_inc(ln_aggr, 1)
                nc.vector.tensor_tensor(mv[:, 1, :], stats[:, :, 1], stats[:, :, 4], ALU.subtract).then_inc(ln_aggr, 1)
                nc.vector.tensor_tensor(mv[:, 2, :], stats[:, :, 2], stats[:, :, 5], ALU.add).then_inc(ln_aggr, 1)
                dve.wait_ge(ln_aggr, b * 6 + 3)
                nc.vector.tensor_scalar(mv[:, 0, :], mv[:, 0, :], 0.5, None, ALU.mult).then_inc(ln_aggr, 1)
                nc.vector.tensor_tensor(mv[:, 1, :], mv[:, 1, :], mv[:, 1, :], ALU.mult).then_inc(ln_aggr, 1)
                nc.vector.tensor_scalar(mv[:, 2, :], mv[:, 2, :], 1.0 / H, LN_EPS, ALU.mult, ALU.add).then_inc(ln_aggr, 1)
                dve.wait_ge(ln_aggr, b * 6 + 6)
                nc.vector.scalar_tensor_tensor(out=rstd[:, 0, :], in0=mv[:, 1, :], scalar=0.25, in1=mv[:, 2, :],
                                               op0=ALU.mult, op1=ALU.add).then_inc(ln_var, 1)
                dve.wait_ge(ln_rstd, b + 1)
                for c in range(TC):
                    nc.vector.tensor_scalar(xt[:, c, :], xt[:, c, :], mv[:, 0, c:c + 1], rstd[:, 1, c:c + 1],
                                            ALU.subtract, ALU.mult).then_inc(xn_done, 1)
                for j in range(KD):
                    dve.wait_ge(u_ps, b * KD + j + 1)
                    for k in range(1, KC):
                        if k == 1:
                            dve.wait_ge(tap0_done, b * KD + j + 1)
                        else:
                            dve.wait_ge(tap_done, (b * KD + j) * (KC - 1) + k - 1)
                        nc.vector.scalar_tensor_tensor(
                            out=acc_r[j % 2][:, k:T], in0=pj[j % 4][:, 0:T - k], scalar=cw[:, j, KC - 1 - k:KC - k],
                            in1=acc_r[j % 2][:, k:T], op0=ALU.mult, op1=ALU.add).then_inc(tap_done, 1)
                    dve.wait_ge(th_done, b * KD + j + 1)
                    nc.vector.scalar_tensor_tensor(out=u[:, j, :], in0=tmp_r[j % 2], scalar=1.0, in1=acc_r[j % 2],
                                                   op0=ALU.add, op1=ALU.mult).then_inc(u_done, 1)
                dve.wait_ge(sq_done, (b + 1) * 2)
                nc.vector.tensor_reduce(ms[:, 0, :, 0:1], nrm[:, :, 0:R], AX.X, ALU.add).then_inc(ms_done, 1)
                nc.vector.tensor_reduce(ms[:, 0, :, 1:3], nrm[:, :, R:F].rearrange("p c (g n) -> p c g n", n=N),
                                        AX.X, ALU.add).then_inc(ms_done, 1)
                dve.wait_ge(ms_done, (b + 1) * 2)
                nc.vector.tensor_scalar(ms[:, 1, :, 0:1], ms[:, 0, :, 0:1], 1.0 / R, RMS_EPS, ALU.mult, ALU.add).then_inc(mse_done, 1)
                nc.vector.tensor_scalar(ms[:, 1, :, 1:3], ms[:, 0, :, 1:3], 1.0 / N, RMS_EPS, ALU.mult, ALU.add).then_inc(mse_done, 1)
                dve.wait_ge(rms_done, b + 1)
                nc.vector.tensor_tensor(nrm[:, :, 0:R], ssm[:, :, 0:R], ms[:, 2, :, 0:1].to_broadcast([P, TC, R]),
                                        ALU.mult).then_inc(nm_done, 1)
                nc.vector.tensor_tensor(nrm[:, :, R:F].rearrange("p c (g n) -> p c g n", n=N),
                                        ssm[:, :, R:F].rearrange("p c (g n) -> p c g n", n=N),
                                        ms[:, 2, :, 1:3].unsqueeze(3).to_broadcast([P, TC, 2, N]),
                                        ALU.mult).then_inc(nm_done, 1)
                dve.wait_ge(nm_done, (b + 1) * 2)
                nc.vector.tensor_tensor(nrm[:, :, :], nrm[:, :, :], lnw[:, :].unsqueeze(1).to_broadcast([P, TC, F]),
                                        ALU.mult).then_inc(nrm_done, 1)
                for j in range(KD):
                    dve.wait_ge(z_ps, b * KD + j + 1)
                    dve.wait_ge(sp_done, b * 3 * KD + 3 * j + 1)
                    if j >= 2:
                        dve.wait_ge(del_done, b * KD + j - 1)
                    nc.vector.tensor_scalar(tmp_r[j % 2], pj[j % 4][:, :], dtb[:, j:j + 1], 0.0,
                                            ALU.add, ALU.max).then_inc(lin_done, 1)

                def add_state(i, c):
                    n, hf = i // HF, i % HF
                    y = yT[:, c, hf * JH * P:(hf + 1) * JH * P]
                    cn = nrm[:, c, R + N + n:R + N + n + 1]
                    dve.wait_ge(hT_ps, b * UNITS * TC + i * TC + c + 1)
                    if n == 0:
                        nc.vector.tensor_scalar(y, hT[c][:, :], cn, None, ALU.mult).then_inc(y_done, 1)
                    else:
                        dve.wait_ge(y_done, b * UNITS * TC + (i - HF) * TC + c + 1)
                        nc.vector.scalar_tensor_tensor(out=y, in0=hT[c][:, :], scalar=cn, in1=y,
                                                       op0=ALU.mult, op1=ALU.add).then_inc(y_done, 1)

                def ffn_tile(t):
                    g, up = pj[2 * t % 4], pj[(2 * t + 1) % 4]
                    dve.wait_ge(fth_done, b * KI + t + 1)
                    nc.vector.scalar_tensor_tensor(out=S[:, t, :], in0=gffn[:, t % TC, :], scalar=1.0, in1=g[:, :],
                                                   op0=ALU.add, op1=ALU.mult).then_inc(fs_done, 1)
                    dve.wait_ge(fu_ps, b * KI + t + 1)
                    dve.wait_ge(fs_done, b * KI + t + 1)
                    nc.vector.scalar_tensor_tensor(out=S[:, t, :], in0=S[:, t, :], scalar=0.5, in1=up[:, :],
                                                   op0=ALU.mult, op1=ALU.mult).then_inc(f_done, 1)

                for i in range(UNITS):
                    for q in range(QH):
                        s = i * QH + q
                        dve.wait_ge(dA_done, b * UNITS * QH + s + 1)
                        dve.wait_ge(dBu_done, b * UNITS * QH + s + 1)
                        if i >= 2 and q == 0:
                            dve.wait_ge(hT_ps, b * UNITS * TC + (i - 1) * TC)
                        nc.vector.tensor_tensor_scan(
                            h[:, i % 2, q * JQ:(q + 1) * JQ, :].rearrange("p j t -> p (j t)"),
                            dA[:, s % S_RING].rearrange("p j t -> p (j t)"),
                            dBu[:, s % S_RING].rearrange("p j t -> p (j t)"),
                            0.0, ALU.mult, ALU.add).then_inc(scan_done, 1)
                        if i > 0:
                            for c in range(q * TC // QH, (q + 1) * TC // QH):
                                add_state(i - 1, c)
                    if i >= 2 and i % 2 == 0 and (i - 2) // 2 < KI:
                        ffn_tile((i - 2) // 2)
                for c in range(TC):
                    add_state(UNITS - 1, c)
                for c in range(TC):
                    dve.wait_ge(gth_done, b * TC + c + 1)
                    nc.vector.scalar_tensor_tensor(out=gffn[:, c, :], in0=gffn[:, c, :], scalar=1.0, in1=pj[c][:, :],
                                                   op0=ALU.add, op1=ALU.mult).then_inc(g_done, 1)
                for j in range(KD):
                    dve.wait_ge(yb_ps, b * KD + j + 1)
                    nc.vector.scalar_tensor_tensor(out=u[:, j, :], in0=u[:, j, :], scalar=dpar[:, j:j + 1],
                                                   in1=pj[2 + j % 2][:, :], op0=ALU.mult, op1=ALU.add).then_inc(yu_done, 1)
                    dve.wait_ge(gtt_done, b * KD + j + 1)
                    nc.vector.scalar_tensor_tensor(out=sg_r[j % 2], in0=sg_r[j % 2], scalar=1.0, in1=pj[j % 2][:, :],
                                                   op0=ALU.add, op1=ALU.mult).then_inc(sg_done, 1)
                for c in range(TC):
                    dve.wait_ge(o_ps, b * TC + c + 1)
                    if c >= 2:
                        dve.wait_ge(out_dma[c % 2], b * TC * 8 + c // 2 * 16)
                    nc.vector.scalar_tensor_tensor(out=o_r[c % 2], in0=pj[c][:, :], scalar=0.25, in1=gffn[:, c, :],
                                                   op0=ALU.mult, op1=ALU.mult).then_inc(og_done, 1)

        @block.tensor
        def _(pe):
            pe.wait_ge(const_in, N_CONST)
            with pe.Fori(0, NB) as b:
                pe.wait_ge(og_done, 1 + b * TC)
                for k in range(KH):
                    for c in range(TC):
                        if k == 0:
                            pe.wait_ge(xn_done, b * TC + c + 1)
                        last = nc.tensor.transpose(pj[k][:, c * P:(c + 1) * P], xt[:, c, k * P:(k + 1) * P], ident[:, :])
                    last.then_inc(xT_ps, 1)
                pe.wait_ge(xT_done, (b + 1) * KH)
                pe.wait_ge(win_in, b * 32 + 16)
                for j in range(KD):
                    if j >= 4:
                        pe.wait_ge(tap_done, (b * KD + j - 3) * (KC - 1))
                    for k in range(KH):
                        last = nc.tensor.matmul(pj[j % 4][:, :], win[:, k, j * P:(j + 1) * P], xnT[:, k, :],
                                                start=(k == 0), stop=(k == KH - 1))
                    last.then_inc(u_ps, 1)
                pe.wait_ge(u_done, (b + 1) * KD)
                for c in range(TC):
                    for j in range(KD):
                        last = nc.tensor.matmul(pj[0][:, c * F:(c + 1) * F], u[:, j, c * P:(c + 1) * P], wx[:, j, :],
                                                start=(j == 0), stop=(j == KD - 1))
                last.then_inc(ssm_ps, 1)
                pe.wait_ge(nrm_done, b + 1)
                for c in range(TC):
                    last = nc.tensor.matmul(pj[1][0:F, c * P:(c + 1) * P], nrm[:, c, :], ident[:, :], start=True, stop=True)
                last.then_inc(dtT_ps, 1)
                pe.wait_ge(dtT_done, b + 1)
                for j in range(KD):
                    if j >= 4:
                        pe.wait_ge(lin_done, b * KD + j - 3)
                    nc.tensor.matmul(pj[j % 4][:, :], wdt[:, j * P:(j + 1) * P], dtB[0:R, :],
                                     start=True, stop=True).then_inc(z_ps, 1)

                def ffn_part(t, part):
                    if part == 0:
                        pe.wait_ge(wgu_in[t % 2], b * 16 * ((KI + 1 - t % 2) // 2) + 16 * (t // 2 + 1))
                        if t < 2:
                            pe.wait_ge(lin_done, b * KD + 6 + 2 * t)
                        else:
                            pe.wait_ge(f_done, b * KI + t - 1)
                    for k in range(KH):
                        last = nc.tensor.matmul(pj[(2 * t + part) % 4][:, :], wgu[:, t % 2, part, k, :], xnT[:, k, :],
                                                start=(k == 0), stop=(k == KH - 1))
                    last.then_inc(fu_ps if part else fg_ps, 1)

                def ffn_down(t):
                    slot, turns = t % WD_RING, (KI + WD_RING - 1 - t % WD_RING) // WD_RING
                    pe.wait_ge(wdn_in[slot], b * 16 * turns + 16 * (t // WD_RING + 1))
                    pe.wait_ge(f_done, b * KI + (KI if t == 0 else t + 1))
                    for c in range(TC):
                        last = nc.tensor.matmul(pj[c][:, :], S[:, t, c * P:(c + 1) * P], wdn[:, slot, :],
                                                start=(t == 0), stop=(t == KI - 1))
                    last.then_inc(dn_used, 1)

                for i in range(UNITS):
                    pe.wait_ge(scan_done, b * UNITS * QH + (i + 1) * QH)
                    for c in range(TC):
                        if i > 0:
                            pe.wait_ge(y_done, b * UNITS * TC + (i - 1) * TC + c + 1)
                        for j in range(JH):
                            last = nc.tensor.transpose(hT[c][:, j * P:(j + 1) * P], h[:, i % 2, j, c * P:(c + 1) * P],
                                                       ident[:, :])
                        last.then_inc(hT_ps, 1)
                    t, part, downs = ffn_slots(i)
                    if t is not None:
                        ffn_part(t, part)
                    for t in downs:
                        ffn_down(t)
                pe.wait_ge(win_in, (b + 1) * 32)
                pe.wait_ge(y_done, (b + 1) * UNITS * TC)
                pe.wait_ge(g_done, (b + 1) * TC)
                for j in range(KD):
                    if j >= 2:
                        pe.wait_ge(sg_done, b * KD + j - 1)
                    for k in range(KH):
                        last = nc.tensor.matmul(pj[j % 2][:, :], win[:, k, j * P:(j + 1) * P], xnT[:, k, :],
                                                start=(k == 0), stop=(k == KH - 1))
                    last.then_inc(gt_ps, 1)
                    for c in range(TC):
                        last = nc.tensor.transpose(pj[2 + j % 2][:, c * P:(c + 1) * P], yT[:, c, j * P:(j + 1) * P],
                                                   ident[:, :])
                    last.then_inc(yb_ps, 1)
                pe.wait_ge(yg_done, 1 + (b + 1) * KD)
                for c in range(TC):
                    for j in range(KD):
                        last = nc.tensor.matmul(pj[c][:, :], u[:, j, c * P:(c + 1) * P], wout[:, j, :],
                                                start=(j == 0), stop=(j == KD - 1))
                    last.then_inc(o_ps, 1)


def kernel(**inputs):
    import concourse.bacc as bacc
    from concourse.bass_utils import run_bass_kernel_spmd

    def get(name):
        return np.asarray(inputs[name])

    def tiles(w):
        return np.ascontiguousarray(w.reshape(-1, P, w.shape[1]).transpose(1, 0, 2))

    def pad(w):
        return np.concatenate([w, np.zeros((KI * P - I, w.shape[1]), w.dtype)])

    w_in = get("L0_attn_W_in").T
    gate_up = [pad(get(f"L0_ffn_{n}")).T.reshape(KH, P, KI, P) for n in ("w_gate", "w_up")]
    arrays = {
        "x": get("L0_attn_hidden_states"),
        "w_in": np.stack([tiles(w_in[:, :D]), tiles(w_in[:, D:])]),
        "w_out": tiles(get("L0_attn_W_out").T),
        "w_x": tiles(get("L0_attn_Wx").T),
        "w_dt": get("L0_attn_Wdt").T,
        "conv_w": tiles(get("L0_attn_conv_w")),
        "conv_b": get("L0_attn_conv_b").reshape(KD, P).T,
        "dt_b": get("L0_attn_dt_bias").reshape(KD, P).T,
        "a_par": tiles(get("L0_attn_A")),
        "d_par": get("L0_attn_D_param").reshape(KD, P).T,
        "ln_w": np.concatenate([get("L0_attn_dt_ln_w"), get("L0_attn_b_ln_w"), get("L0_attn_c_ln_w")]),
        "w_gu": np.stack(gate_up).transpose(3, 2, 0, 1, 4),
        "w_dn": pad(get("L0_ffn_w_down").T).reshape(KI, P, H),
        "ident": np.eye(P, dtype=np.float32),
    }
    nc = bacc.Bacc("TRN2", target_bir_lowering=False, num_devices=1)
    args = []
    for name in arrays:
        arrays[name] = np.ascontiguousarray(arrays[name])
        args.append(nc.dram_tensor(name, arrays[name].shape, mybir.dt.float32, kind="ExternalInput").ap())
    out = nc.dram_tensor("out", (NB, T, H), mybir.dt.float32, kind="ExternalOutput").ap()
    build(nc, *args, out)
    r = run_bass_kernel_spmd(nc, [arrays], core_ids=[0])
    return r.results[0]["out"]
```

```python
import numpy as np
import concourse.bass as bass
from concourse import mybir
from concourse.alu_op_type import AluOpType as ALU
from contextlib import ExitStack

NB, T, H, D, N, R, KC, I = 4, 512, 512, 1024, 16, 32, 4, 1376
P = 128
KH, KD, KI, TC = H // P, D // P, -(-I // P), T // P
HF = 2
JH = KD // HF
JQ = 2
QH = JH // JQ
UNITS = N * HF
F = R + 2 * N
LN_EPS, RMS_EPS = 1e-5, 1e-6
W_RING, HI_RING, B_RING, S_RING, LOG_RING = 2, 2, 2, 3, 6
G = R + 1
FN = F + 1

Z_MAX = 88.0

E_OUT, E_GATE, E_FFN, E_U, E_DOWN = 0, KD // 2, KD, KD + KI, KD + KI + KD // 2
N_OUT, N_DOWN = KD // 2, -(-KI // 2)
ENTRIES = E_DOWN + N_DOWN
SPLITS = E_DOWN - E_GATE
AT_OUT, AT_GATE, AT_FFN = 0, KD // 2, KD
AT_XT = AT_FFN + KI
AT_U = AT_XT + 1
AT_DOWN = AT_U + KD // 2
AT_SSM, AT_DTT = AT_DOWN + 3, UNITS - 1
AT_LN = AT_FFN + 2
ENTRY_AT = ([(AT_OUT + e, E_OUT + e) for e in range(KD // 2)] + [(AT_GATE + e, E_GATE + e) for e in range(KD // 2)]
            + [(AT_FFN + e, E_FFN + e) for e in range(KI)] + [(AT_U + e, E_U + e) for e in range(KD // 2)]
            + [(AT_DOWN + e, E_DOWN + e) for e in range(ENTRIES - E_DOWN)])
SPLIT_AT = {**{AT_GATE + e: E_GATE + e for e in range(KD // 2 + KI)}, **{AT_U + e - (e < HI_RING): E_U + e for e in range(KD // 2)}}


def build(nc, x, w_ring, w_x, w_dt, conv_w, conv_b, a_par, d_par, ln_w, ident_d, out):
    fp32 = mybir.dt.float32
    fp32r = mybir.dt.float32r
    ACT = mybir.ActivationFunctionType
    AX = mybir.AxisListType
    ctx = ExitStack()
    with ctx:
        def sb(name, shape, dtype=fp32):
            return ctx.enter_context(nc.sbuf_tensor("sb_" + name, shape, dtype))

        def ps(name):
            return ctx.enter_context(nc.psum_tensor(name, [P, T], fp32))

        def sem(name):
            return ctx.enter_context(nc.semaphore(name))

        wx = sb("wx", [P, KD, F])
        wdt = sb("wdt", [G, D])
        cw = sb("cw", [P, KD, KC])
        cb = sb("cb", [P, KD])
        apar = sb("apar", [P, KD, N])
        dpar = sb("dpar", [P, KD])
        lnw = sb("lnw", [P, F])
        ident = sb("ident", [P, P])
        half = sb("half", [P, 3 * TC])
        ring = sb("ring", [P, W_RING, 2, H])
        w_hi = sb("w_hi", [P, HI_RING, 2, H], fp32r)
        w_lo = sb("w_lo", [P, HI_RING, 2, H], fp32r)
        x_hi = sb("x_hi", [P, KH, T], fp32r)
        x_lo = sb("x_lo", [P, KH, T], fp32r)
        un = sb("un", [P, KD, T])
        u = sb("u", [P, KD, T])
        delta = sb("delta", [P, KD, T])
        v = sb("v", [P, KD, T])
        sgate = sb("sgate", [P, KD, T])
        ssm = sb("ssm", [P, TC, F])
        nrm = sb("nrm", [P, TC, FN])
        cs = sb("cs", [P, TC, N])
        dtB = sb("dtB", [G + N, T])
        bb = sb("bb", [P, B_RING, T])
        dA = sb("dA", [P, S_RING, JQ, T])
        dBu = sb("dBu", [P, S_RING, JQ, T])
        h = sb("h", [P, 2, JH, T])
        yT = sb("yT", [P, TC, D])
        gffn = sb("gffn", [P, TC, H])
        S = sb("S", [P, KI, T])
        stats = sb("stats", [P, TC, 6])
        mv = sb("mv", [P, 3, TC])
        rstd = sb("rstd", [P, 2, TC])
        ms = sb("ms", [P, 3, TC, 3])
        xt = un[:, 0:TC, :]
        xres = S[:, 0:TC, :]
        o = S[:, TC:2 * TC, :]
        log_r = [S[:, TC + r, :] for r in range(LOG_RING)]

        pj = [ps(f"pj{i}") for i in range(4)]
        aux = [ps(f"aux{i}") for i in range(2)]
        hT = [ps(f"hT{i}") for i in range(2)]
        xT_bank = [aux[0], aux[1], pj[2], pj[3]]
        yb_bank = [hT[0], hT[1], aux[0], aux[1]]
        u_bank = [pj[j % 4] for j in range(6)] + aux
        gate_bank = aux + pj + aux
        ssm_bank0 = hT + pj[2:]
        b_dram = nc.dram_tensor("b_rows", [N, T], fp32, kind="Internal").ap()

        const_in = sem("const_in")
        init_done = sem("init_done")
        half_done = sem("half_done")
        w_in = [sem(f"w_in{r}") for r in range(W_RING)]
        x_in = sem("x_in")
        ln_stat = sem("ln_stat")
        ln_aggr = sem("ln_aggr")
        ln_var = sem("ln_var")
        ln_rstd = sem("ln_rstd")
        xn_done = sem("xn_done")
        xT_ps = sem("xT_ps")
        xh_done = sem("xh_done")
        xT_done = sem("xT_done")
        hi_done = sem("hi_done")
        lo_done = sem("lo_done")
        u_ps = sem("u_ps")
        tap0_done = sem("tap0_done")
        tap_done = sem("tap_done")
        th_done = sem("th_done")
        th1_done = sem("th1_done")
        u_done = sem("u_done")
        ssm_ps = sem("ssm_ps")
        sq_done = sem("sq_done")
        ms_done = sem("ms_done")
        mse_done = sem("mse_done")
        rms_done = sem("rms_done")
        nm_done = sem("nm_done")
        nrm_done = sem("nrm_done")
        dtT_ps = sem("dtT_ps")
        dtT_done = sem("dtT_done")
        cs_done = sem("cs_done")
        b_out = sem("b_out")
        b_in = [sem(f"b_in{r}") for r in range(B_RING)]
        z_ps = sem("z_ps")
        sp_done = sem("sp_done")
        del_done = sem("del_done")
        v_done = sem("v_done")
        ud_done = sem("ud_done")
        dA_done = sem("dA_done")
        dBu_done = sem("dBu_done")
        scan_done = sem("scan_done")
        hT_ps = sem("hT_ps")
        y_done = sem("y_done")
        gt_ps = sem("gt_ps")
        gtt_done = sem("gtt_done")
        sg_done = sem("sg_done")
        fg_ps = sem("fg_ps")
        fu_ps = sem("fu_ps")
        fth_done = sem("fth_done")
        fs_done = sem("fs_done")
        f_done = sem("f_done")
        dn_used = sem("dn_used")
        gth_done = sem("gth_done")
        g_done = sem("g_done")
        yb_ps = sem("yb_ps")
        yu_done = sem("yu_done")
        yg_done = sem("yg_done")
        out_used = sem("out_used")
        og_done = sem("og_done")
        o_done = sem("o_done")
        xr_in = sem("xr_in")
        out_dma = sem("out_dma")

        consts = [(wx, w_x), (wdt, w_dt), (cw, conv_w), (cb, conv_b), (apar, a_par), (dpar, d_par), (ident, ident_d)]
        N_CONST = 16 * (len(consts) + 1)
        SU = UNITS * QH

        def loaded(b, k, no_u=False):
            a_seq = len(range(k % W_RING, ENTRIES, W_RING))
            u_seq = len([e for e in range(E_U, E_DOWN) if e % W_RING == k % W_RING])
            return 16 * (b * a_seq + k // W_RING + 1 - (u_seq if no_u else 0))

        def split(b, k):
            return KD // 2 + b * SPLITS + k - E_GATE + 1

        def wait_used(eng, b, k, first):
            if k < E_GATE and first or E_GATE <= k < E_DOWN:
                eng.wait_ge(lo_done, split(b, k) if k >= E_GATE else k + 1)
            elif k < E_GATE:
                eng.wait_ge(out_used, (b - 1) * N_OUT + k + 1)
            else:
                eng.wait_ge(dn_used, b * N_DOWN + k - E_DOWN + 1)

        def sequences(eng, body):
            body(0, True, False)
            with eng.Fori(1, NB - 1) as b:
                body(b, False, False)
            body(NB - 1, False, True)

        def rows(dram, b):
            return dram[bass.ds(b, 1), :, :].rearrange("o (c p) h -> p (o c) h", p=P)

        block = ctx.enter_context(nc.Block())

        @block.sync
        def _(sp):
            def load(k, source):
                sp.dma_start(ring[:, k % W_RING], w_ring[source]).then_inc(w_in[k % W_RING], 16)

            def b_rows(c):
                sp.wait_ge(dtT_done, c + 1)
                sp.dma_start(b_dram, dtB[G:G + N, :]).then_inc(b_out, 16)
                sp.wait_ge(b_out, (c + 1) * 16)
                for n in range(B_RING):
                    sp.dma_start(bb[:, n, :], b_dram[n, :].partition_broadcast(P)).then_inc(b_in[n], 16)

            sp.dma_start(xt, rows(x, 0)).then_inc(x_in, 16)
            for dst, src in consts:
                sp.dma_start(dst[:], src).then_inc(const_in, 16)
            sp.dma_start(lnw[:, :], ln_w.partition_broadcast(P)).then_inc(const_in, 16)
            for e in range(KD // 2):
                if e >= W_RING:
                    sp.wait_ge(lo_done, e - W_RING + 1)
                load(e, E_U + e)
            b_rows(0)

            def sequence(b, first, last):
                entry_at = dict(ENTRY_AT)
                for i in range(UNITS):
                    k = entry_at.get(i)
                    if k is not None and not (last and E_U <= k < E_DOWN) and not (first and k + W_RING < E_GATE):
                        nxt = k + W_RING
                        while last and E_U <= nxt < E_DOWN:
                            nxt += W_RING
                        if nxt < ENTRIES:
                            wait_used(sp, b, k, first)
                            load(nxt, nxt)
                    if i % HF == HF - 1 and i // HF + B_RING < N:
                        m = i // HF + B_RING
                        sp.wait_ge(dBu_done, b * SU + (i + 1) * QH)
                        sp.dma_start(bb[:, m % B_RING, :], b_dram[m, :].partition_broadcast(P)).then_inc(b_in[m % B_RING], 16)
                for k in range(ENTRIES - W_RING, ENTRIES):
                    wait_used(sp, b, k, first)
                    load(k % W_RING, E_OUT + k % W_RING)
                sp.dma_start(xres, rows(x, b)).then_inc(xr_in, 16)
                if not last:
                    b_rows(b + 1)

            sequences(sp, sequence)
            for k in range(W_RING, N_OUT):
                wait_used(sp, NB, k - W_RING, False)
                load(k, E_OUT + k)
            sp.wait_ge(o_done, NB * TC)
            sp.dma_start(rows(out, NB - 1), o).then_inc(out_dma, 16)
            sp.wait_ge(out_dma, NB * 16)

        @block.scalar
        def _(act):
            act.wait_ge(const_in, N_CONST)
            act.wait_ge(init_done, 4)
            act.wait_ge(half_done, 2)

            def round_x(c):
                for k in range(KH):
                    act.wait_ge(xT_ps, c * KH + k + 1)
                    nc.scalar.copy(x_hi[:, k, :], xT_bank[k][:, :]).then_inc(xh_done, 1)

            def round_w(slot, k):
                nc.scalar.copy(w_hi[:, (k - E_GATE) % HI_RING], ring[:, slot]).then_inc(hi_done, 1)

            def round_entry(b, k):
                act.wait_ge(w_in[k % W_RING], loaded(b, k))
                before = k - HI_RING
                if before < E_GATE:
                    act.wait_ge(u_ps, (b + 1) * KD)
                elif before < E_FFN:
                    act.wait_ge(gt_ps, b * KD + 2 * (before - E_GATE + 1))
                elif before < E_U:
                    act.wait_ge(fu_ps, b * KI + before - E_FFN + 1)
                else:
                    act.wait_ge(u_ps, (b + 1) * KD + 2 * (before - E_U + 1))
                round_w(k % W_RING, k)

            def round_first(e):
                act.wait_ge(w_in[e % W_RING], 16 * (e // W_RING + 1))
                if e >= HI_RING:
                    act.wait_ge(u_ps, 2 * (e - HI_RING + 1))
                round_w(e % W_RING, E_U + e)

            def first_tap(c, j):
                act.wait_ge(u_ps, c * KD + j + 1)
                nc.scalar.activation(un[:, j, :], u_bank[j][:, :], ACT.Identity, bias=cb[:, j:j + 1],
                                     scale=cw[:, j, KC - 1:KC]).then_inc(tap0_done, 1)

            def conv_tanh(c, j):
                act.wait_ge(tap_done, (c * KD + j + 1) * (KC - 1))
                if j >= TC:
                    act.wait_ge(u_done, c * KD + j - TC + 1)
                nc.scalar.activation(gffn[:, j % TC, :], un[:, j, :], ACT.Tanh).then_inc(th_done, 1)

            def conv_plus1(c, j):
                act.wait_ge(th_done, c * KD + j + 1)
                nc.scalar.activation(gffn[:, j % TC, :], gffn[:, j % TC, :], ACT.Copy, bias=1.0).then_inc(th1_done, 1)

            def squares(c):
                act.wait_ge(ssm_ps, c + 1)
                copy_squares(slice(0, TC), aux[0][:, 0:TC * F].rearrange("p (c f) -> p c f", f=F))

            def copy_squares(t, p_ssm):
                nc.scalar.copy(ssm[:, t, :], p_ssm)
                nc.scalar.activation(nrm[:, t, 0:R], p_ssm[:, :, 0:R], ACT.Square)
                nc.scalar.activation(nrm[:, t, G:FN], p_ssm[:, :, R:F], ACT.Square).then_inc(sq_done, 1)

            def hand_dt(c):
                act.wait_ge(dtT_ps, c + 1)
                if not (isinstance(c, int) and c == 0):
                    act.wait_ge(dBu_done, c * SU)
                nc.scalar.copy(dtB[:, :], aux[1][0:G + N, :]).then_inc(dtT_done, 1)
                nc.scalar.preload_act_table_set("natural_log_exp_and_others")

            def softplus(c, p):
                pair = (2 * p, 2 * p + 1)
                for j in pair:
                    act.wait_ge(z_ps, c * KD + j + 1)
                    if j >= LOG_RING:
                        act.wait_ge(del_done, c * KD + j - LOG_RING + 1)
                    nc.scalar.activation(log_r[j % LOG_RING], pj[j % 4][:, :], ACT.Exp).then_inc(sp_done, 1)
                for j in pair:
                    act.wait_ge(sp_done, c * 2 * KD + 4 * p + j % 2 + 1)
                    nc.scalar.activation(log_r[j % LOG_RING], log_r[j % LOG_RING], ACT.Ln, bias=1.0).then_inc(sp_done, 1)

            for e in range(HI_RING):
                round_first(e)
            round_x(0)
            for j in range(KD + 1):
                if j < KD:
                    first_tap(0, j)
                    if j % 2 == 1 and j // 2 + HI_RING < KD // 2:
                        round_first(j // 2 + HI_RING)
                if j > 0:
                    conv_tanh(0, j - 1)
                    conv_plus1(0, j - 1)
            act.wait_ge(ssm_ps, 1)
            for t in range(TC):
                copy_squares(slice(t, t + 1), ssm_bank0[t][:, 0:F].unsqueeze(1))
            hand_dt(0)

            def sequence(b, first, last):
                def decay(i, q):
                    n, hf, s = i // HF, i % HF, i * QH + q
                    if n == 0:
                        act.wait_ge(del_done, b * KD + hf * JH + (q + 1) * JQ)
                    if s >= S_RING:
                        act.wait_ge(scan_done, b * SU + s - S_RING + 1)
                    for e in range(JQ):
                        j = hf * JH + q * JQ + e
                        done = nc.scalar.activation(dA[:, s % S_RING, e, 1:T], delta[:, j, 1:T], ACT.Exp,
                                                    scale=apar[:, j, n:n + 1])
                    done.then_inc(dA_done, 1)

                def side(i):
                    e = i - AT_GATE - 1
                    if 0 <= e < KD // 2:
                        if e == 0 and not first:
                            act.wait_ge(out_used, b * N_OUT)
                        for j in (2 * e, 2 * e + 1):
                            nc.scalar.activation(u[:, j, :], un[:, j, :], ACT.Copy,
                                                 scale=dpar[:, j:j + 1]).then_inc(ud_done, 1)
                    if i == AT_GATE + 5 and not last:
                        act.wait_ge(ud_done, (b + 1) * KD)
                        act.wait_ge(v_done, (b + 1) * (KD // JQ))
                        act.dma_start(xt, rows(x, b + 1)).then_inc(x_in, 16)
                    if i == AT_FFN + 3 and not first:
                        act.wait_ge(o_done, b * TC)
                        act.dma_start(rows(out, b - 1), o).then_inc(out_dma, 16)
                    e = i - AT_GATE - 2
                    if 0 <= e < KD // 2:
                        for j in (2 * e, 2 * e + 1):
                            act.wait_ge(gt_ps, b * KD + j + 1)
                            nc.scalar.activation(sgate[:, j, :], gate_bank[j][:, :], ACT.Tanh, scale=0.5).then_inc(gtt_done, 1)
                    t = i - AT_FFN - 2
                    if 0 <= t < KI:
                        act.wait_ge(fg_ps, b * KI + t + 1)
                        if t >= TC:
                            act.wait_ge(fs_done, b * KI + t - TC + 1)
                        nc.scalar.activation(gffn[:, t % TC, :], pj[2 * t % 4][:, :], ACT.Tanh, scale=0.5).then_inc(fth_done, 1)
                    e = i - AT_U - 4
                    if 0 <= e < KD // 2 and not last:
                        if e == 0:
                            act.wait_ge(fs_done, (b + 1) * KI)
                        for j in (2 * e, 2 * e + 1):
                            conv_tanh(b + 1, j)
                        for j in (2 * e, 2 * e + 1):
                            conv_plus1(b + 1, j)
                    e = i - AT_U - 2
                    if 0 <= e < KD // 2 and not last:
                        for j in (2 * e, 2 * e + 1):
                            first_tap(b + 1, j)
                    if i == AT_SSM + 3 and not last:
                        squares(b + 1)
                    if i == UNITS - 1:
                        act.wait_ge(fs_done, (b + 1) * KI)
                        if not last:
                            act.wait_ge(u_done, (b + 2) * KD)
                        act.wait_ge(dn_used, (b + 1) * N_DOWN)
                        for c in range(TC):
                            nc.scalar.activation(gffn[:, c, :], pj[c][:, :], ACT.Tanh, scale=0.5).then_inc(gth_done, 1)

                for i in range(UNITS):
                    for q in range(QH):
                        if i == 0 and q == 0:
                            softplus(b, 0)
                        if i < HF and i * QH + q + 1 < KD // JQ:
                            softplus(b, i * QH + q + 1)
                        decay(i, q)
                        if q == 0:
                            side(i)
                    if i in SPLIT_AT and not (last and SPLIT_AT[i] >= E_U):
                        round_entry(b, SPLIT_AT[i])
                    if i == AT_XT + 1 and not last:
                        round_x(b + 1)
                if not last:
                    hand_dt(b + 1)

            sequences(act, sequence)

        @block.gpsimd
        def _(pool):
            pool.wait_ge(init_done, 4)

            def power_ln(c):
                pool.wait_ge(ln_var, c + 1)
                nc.gpsimd.tensor_tensor(rstd[:, 1, :], rstd[:, 0, :], half[:, 0:TC], ALU.pow).then_inc(ln_rstd, 1)

            def power_rms(c):
                pool.wait_ge(mse_done, (c + 1) * 2)
                nc.gpsimd.tensor_tensor(ms[:, 2].rearrange("p c g -> p (c g)"), ms[:, 1].rearrange("p c g -> p (c g)"),
                                        half[:, :], ALU.pow).then_inc(rms_done, 1)

            def rest_w(slot, k, count):
                pool.wait_ge(hi_done, count)
                nc.gpsimd.tensor_tensor(w_lo[:, (k - E_GATE) % HI_RING], ring[:, slot], w_hi[:, (k - E_GATE) % HI_RING].bitcast(fp32),
                                        ALU.subtract).then_inc(lo_done, 1)

            def times_gate(b, first_j, end_j):
                for j in range(first_j, end_j):
                    pool.wait_ge(yu_done, b * KD + j + 1)
                    nc.gpsimd.tensor_tensor(u[:, j, :], u[:, j, :], sgate[:, j, :], ALU.mult).then_inc(yg_done, 1)

            def conv_silu(c, j):
                pool.wait_ge(th1_done, c * KD + j + 1)
                nc.gpsimd.tensor_tensor(un[:, j, :], gffn[:, j % TC, :], un[:, j, :], ALU.mult).then_inc(u_done, 1)

            power_ln(0)
            for e in range(HI_RING):
                rest_w(e % W_RING, E_U + e, e + 1)
            for j in range(KD):
                e = j // 2 + HI_RING
                if j % 2 == 0 and e < KD // 2:
                    rest_w(e % W_RING, E_U + e, e + 1)
                conv_silu(0, j)
            power_rms(0)

            def sequence(b, first, last):
                for i in range(UNITS):
                    n, hf = i // HF, i % HF
                    if i == AT_LN + TC + 2 and not last:
                        power_ln(b + 1)
                    if hf == 0:
                        pool.wait_ge(b_in[n % B_RING], b * 16 * (N // B_RING) + 16 * (n // B_RING + 1))
                    for q in range(QH):
                        s = i * QH + q
                        j = hf * JH + q * JQ
                        if n == 0:
                            pool.wait_ge(v_done, b * (KD // JQ) + j // JQ + 1)
                        if s >= S_RING:
                            pool.wait_ge(scan_done, b * SU + s - S_RING + 1)
                        nc.gpsimd.tensor_tensor(dBu[:, s % S_RING, :, :], v[:, j:j + JQ, :],
                                                bb[:, n % B_RING, :].unsqueeze(1).to_broadcast([P, JQ, T]),
                                                ALU.mult).then_inc(dBu_done, 1)
                    if i in SPLIT_AT and not (last and SPLIT_AT[i] >= E_U):
                        k = SPLIT_AT[i]
                        rest_w(k % W_RING, k, split(b, k))
                    e = i - AT_U - 4
                    if 0 <= e < KD // 2 and not last:
                        for j in (2 * e, 2 * e + 1):
                            conv_silu(b + 1, j)
                    if i < HF and not first:
                        times_gate(b - 1, *((2, JH) if i == 0 else (JH, KD)))
                if not last:
                    power_rms(b + 1)
                times_gate(b, 0, 2)

            sequences(pool, sequence)
            times_gate(NB - 1, 2, KD)

        @block.vector
        def _(dve):
            nc.vector.memset(half[:, :], -0.5).then_inc(init_done, 1)
            nc.vector.memset(nrm[:, :, R:G], 1.0).then_inc(init_done, 1)
            for e in range(JQ):
                nc.vector.memset(dA[:, :, e, 0:1], 0.0).then_inc(init_done, 1)

            def ln_stats(c, t):
                if t == 0:
                    dve.wait_ge(x_in, (c + 1) * 16)
                nc.vector.bn_stats(stats[:, t, :], xt[:, t, :]).then_inc(ln_stat, 1)

            def ln_variance(c):
                dve.wait_ge(ln_stat, (c + 1) * TC)
                nc.vector.tensor_tensor(mv[:, 0, :], stats[:, :, 1], stats[:, :, 4], ALU.add).then_inc(ln_aggr, 1)
                nc.vector.tensor_tensor(mv[:, 1, :], stats[:, :, 1], stats[:, :, 4], ALU.subtract).then_inc(ln_aggr, 1)
                nc.vector.tensor_tensor(mv[:, 2, :], stats[:, :, 2], stats[:, :, 5], ALU.add).then_inc(ln_aggr, 1)
                dve.wait_ge(ln_aggr, c * 6 + 3)
                nc.vector.tensor_scalar(mv[:, 0, :], mv[:, 0, :], 0.5, None, ALU.mult).then_inc(ln_aggr, 1)
                nc.vector.tensor_tensor(mv[:, 1, :], mv[:, 1, :], mv[:, 1, :], ALU.mult).then_inc(ln_aggr, 1)
                nc.vector.tensor_scalar(mv[:, 2, :], mv[:, 2, :], 1.0 / H, LN_EPS, ALU.mult, ALU.add).then_inc(ln_aggr, 1)
                dve.wait_ge(ln_aggr, c * 6 + 6)
                nc.vector.scalar_tensor_tensor(out=rstd[:, 0, :], in0=mv[:, 1, :], scalar=0.25, in1=mv[:, 2, :],
                                               op0=ALU.mult, op1=ALU.add).then_inc(ln_var, 1)

            def ln_apply(c, t):
                if t == 0:
                    dve.wait_ge(ln_rstd, c + 1)
                nc.vector.tensor_scalar(xt[:, t, :], xt[:, t, :], mv[:, 0, t:t + 1], rstd[:, 1, t:t + 1],
                                        ALU.subtract, ALU.mult).then_inc(xn_done, 1)

            def rest_x(c, first_k, end_k):
                for k in range(first_k, end_k):
                    dve.wait_ge(xh_done, c * KH + k + 1)
                    nc.vector.tensor_tensor(x_lo[:, k, :], xT_bank[k][:, :], x_hi[:, k, :].bitcast(fp32),
                                            ALU.subtract).then_inc(xT_done, 1)

            def taps(c, j):
                acc = un[:, j, :]
                for k in range(1, KC):
                    if k == 1:
                        dve.wait_ge(tap0_done, c * KD + j + 1)
                    else:
                        dve.wait_ge(tap_done, (c * KD + j) * (KC - 1) + k - 1)
                    nc.vector.scalar_tensor_tensor(
                        out=acc[:, k:T], in0=u_bank[j][:, 0:T - k], scalar=cw[:, j, KC - 1 - k:KC - k],
                        in1=acc[:, k:T], op0=ALU.mult, op1=ALU.add).then_inc(tap_done, 1)

            def rms_squares(c):
                dve.wait_ge(sq_done, c + TC)
                nc.vector.tensor_reduce(ms[:, 0, :, 0:1], nrm[:, :, 0:R], AX.X, ALU.add).then_inc(ms_done, 1)
                nc.vector.tensor_reduce(ms[:, 0, :, 1:3], nrm[:, :, G:FN].rearrange("p c (g n) -> p c g n", n=N),
                                        AX.X, ALU.add).then_inc(ms_done, 1)
                dve.wait_ge(ms_done, (c + 1) * 2)
                nc.vector.tensor_scalar(ms[:, 1, :, 0:1], ms[:, 0, :, 0:1], 1.0 / R, RMS_EPS, ALU.mult, ALU.add).then_inc(mse_done, 1)
                nc.vector.tensor_scalar(ms[:, 1, :, 1:3], ms[:, 0, :, 1:3], 1.0 / N, RMS_EPS, ALU.mult, ALU.add).then_inc(mse_done, 1)

            def rms_apply(c):
                dve.wait_ge(rms_done, c + 1)
                nc.vector.tensor_tensor(ssm[:, :, 0:R], ssm[:, :, 0:R], ms[:, 2, :, 0:1].to_broadcast([P, TC, R]),
                                        ALU.mult).then_inc(nm_done, 1)
                bc = ssm[:, :, R:F].rearrange("p c (g n) -> p c g n", n=N)
                nc.vector.tensor_tensor(bc, bc, ms[:, 2, :, 1:3].unsqueeze(3).to_broadcast([P, TC, 2, N]),
                                        ALU.mult).then_inc(nm_done, 1)
                dve.wait_ge(nm_done, (c + 1) * 2)
                w = lnw[:, :].unsqueeze(1)
                nc.vector.tensor_tensor(nrm[:, :, 0:R], ssm[:, :, 0:R], w[:, :, 0:R].to_broadcast([P, TC, R]),
                                        ALU.mult).then_inc(nrm_done, 1)
                nc.vector.tensor_tensor(nrm[:, :, G:FN], ssm[:, :, R:F], w[:, :, R:F].to_broadcast([P, TC, 2 * N]),
                                        ALU.mult).then_inc(nrm_done, 1)

            def hand_c(c):
                dve.wait_ge(nrm_done, (c + 1) * 2)
                nc.vector.tensor_copy(cs[:, :, :], nrm[:, :, G + N:FN]).then_inc(cs_done, 1)

            def step_size(c, j):
                dve.wait_ge(sp_done, c * 2 * KD + 4 * (j // 2) + 3 + j % 2)
                nc.vector.scalar_tensor_tensor(out=delta[:, j, :], in0=log_r[j % LOG_RING], scalar=Z_MAX, in1=pj[j % 4][:, :],
                                               op0=ALU.min, op1=ALU.max).then_inc(del_done, 1)

            def inputs(c, p):
                j = p * JQ
                dve.wait_ge(del_done, c * KD + j + JQ)
                nc.vector.tensor_tensor(v[:, j:j + JQ, :], delta[:, j:j + JQ, :], un[:, j:j + JQ, :],
                                        ALU.mult).then_inc(v_done, 1)

            def times_g(b, part):
                if part == 0:
                    dve.wait_ge(out_used, (b + 1) * N_OUT)
                for c in range(part * TC // 2, (part + 1) * TC // 2):
                    nc.vector.scalar_tensor_tensor(out=o[:, c, :], in0=pj[c][:, :], scalar=0.25, in1=gffn[:, c, :],
                                                   op0=ALU.mult, op1=ALU.mult).then_inc(og_done, 1)

            def residual(b, c):
                if c == 0:
                    dve.wait_ge(xr_in, (b + 1) * 16)
                dve.wait_ge(og_done, b * TC + c + 1)
                nc.vector.tensor_tensor(o[:, c, :], o[:, c, :], xres[:, c, :], ALU.add).then_inc(o_done, 1)

            for t in range(TC):
                ln_stats(0, t)
            ln_variance(0)
            dve.wait_ge(const_in, N_CONST)
            nc.vector.tensor_scalar(cw[:, :, :], cw[:, :, :], 0.5, None, ALU.mult).then_inc(half_done, 1)
            nc.vector.tensor_scalar(cb[:, :], cb[:, :], 0.5, None, ALU.mult).then_inc(half_done, 1)
            for t in range(TC):
                ln_apply(0, t)
            rest_x(0, 0, KH)
            dve.wait_ge(half_done, 2)
            for j in range(KD):
                taps(0, j)
            rms_squares(0)
            rms_apply(0)
            hand_c(0)
            for j in range(JH):
                step_size(0, j)
                if j % JQ == JQ - 1:
                    inputs(0, j // JQ)

            def sequence(b, first, last):
                def add_state(i, c):
                    n, hf = i // HF, i % HF
                    y = yT[:, c, hf * JH * P:(hf + 1) * JH * P]
                    cn = cs[:, c, n:n + 1]
                    dve.wait_ge(hT_ps, b * UNITS * TC + i * TC + c + 1)
                    if n == 0:
                        dve.wait_ge(cs_done, b + 1)
                        nc.vector.tensor_scalar(y, hT[c % 2][:, :], cn, None, ALU.mult).then_inc(y_done, 1)
                    else:
                        dve.wait_ge(y_done, b * UNITS * TC + (i - HF) * TC + c + 1)
                        nc.vector.scalar_tensor_tensor(out=y, in0=hT[c % 2][:, :], scalar=cn, in1=y,
                                                       op0=ALU.mult, op1=ALU.add).then_inc(y_done, 1)

                def ffn_tile(t, part):
                    if part == 0:
                        if t == 0 and not first:
                            dve.wait_ge(o_done, b * TC)
                        if t == TC and not first:
                            dve.wait_ge(out_dma, b * 16)
                        dve.wait_ge(fth_done, b * KI + t + 1)
                        nc.vector.scalar_tensor_tensor(out=S[:, t, :], in0=gffn[:, t % TC, :], scalar=1.0, in1=pj[2 * t % 4][:, :],
                                                       op0=ALU.add, op1=ALU.mult).then_inc(fs_done, 1)
                    else:
                        dve.wait_ge(fu_ps, b * KI + t + 1)
                        dve.wait_ge(fs_done, b * KI + t + 1)
                        nc.vector.scalar_tensor_tensor(out=S[:, t, :], in0=S[:, t, :], scalar=0.5, in1=pj[(2 * t + 1) % 4][:, :],
                                                       op0=ALU.mult, op1=ALU.mult).then_inc(f_done, 1)

                def side(i, part):
                    if i == AT_GATE + 1 and not first:
                        times_g(b - 1, part)
                    if 0 <= i - AT_GATE - 2 < TC and part == 1 and not first:
                        residual(b - 1, i - AT_GATE - 2)
                    e = i - AT_GATE - 2
                    if 0 <= e < KD // 2:
                        j = 2 * e + part
                        dve.wait_ge(gtt_done, b * KD + j + 1)
                        nc.vector.scalar_tensor_tensor(out=sgate[:, j, :], in0=sgate[:, j, :], scalar=1.0,
                                                       in1=gate_bank[j][:, :], op0=ALU.add, op1=ALU.mult).then_inc(sg_done, 1)
                    t = i - AT_FFN - 2
                    if 0 <= t < KI:
                        ffn_tile(t, part)
                    if not last:
                        if 0 <= i - AT_LN < TC and part == 1:
                            ln_stats(b + 1, i - AT_LN)
                        if i == AT_LN + TC and part == 1:
                            ln_variance(b + 1)
                        if 0 <= i - AT_LN - TC - 2 < 2:
                            ln_apply(b + 1, 2 * (i - AT_LN - TC - 2) + part)
                        if i == AT_XT + 1:
                            rest_x(b + 1, 2 * part, 2 * part + 2)
                        e = i - AT_U - 2
                        if 0 <= e < KD // 2:
                            taps(b + 1, 2 * e + part)
                        if i == AT_SSM + 3 and part == 0:
                            rms_squares(b + 1)
                        if i == AT_SSM + 4 and part == 0:
                            rms_apply(b + 1)
                    if i == UNITS - 1:
                        for c in range(part * TC // 2, (part + 1) * TC // 2):
                            dve.wait_ge(gth_done, b * TC + c + 1)
                            nc.vector.scalar_tensor_tensor(out=gffn[:, c, :], in0=gffn[:, c, :], scalar=1.0, in1=pj[c][:, :],
                                                           op0=ALU.add, op1=ALU.mult).then_inc(g_done, 1)

                for i in range(UNITS):
                    for q in range(QH):
                        s = i * QH + q
                        dve.wait_ge(dA_done, b * SU + s + 1)
                        dve.wait_ge(dBu_done, b * SU + s + 1)
                        if i >= 2 and q == 0:
                            dve.wait_ge(hT_ps, b * UNITS * TC + (i - 1) * TC)
                        nc.vector.tensor_tensor_scan(
                            h[:, i % 2, q * JQ:(q + 1) * JQ, :].rearrange("p j t -> p (j t)"),
                            dA[:, s % S_RING].rearrange("p j t -> p (j t)"),
                            dBu[:, s % S_RING].rearrange("p j t -> p (j t)"),
                            0.0, ALU.mult, ALU.add).then_inc(scan_done, 1)
                        if i == 0 and q == QH - 1:
                            for j in range(JH, KD):
                                step_size(b, j)
                                if j % JQ == JQ - 1:
                                    inputs(b, j // JQ)
                        if i > 0:
                            for c in range(q * TC // QH, (q + 1) * TC // QH):
                                add_state(i - 1, c)
                        side(i, q)
                for c in range(TC):
                    add_state(UNITS - 1, c)
                if not last:
                    dve.wait_ge(y_done, (b + 1) * UNITS * TC)
                    hand_c(b + 1)
                dve.wait_ge(ud_done, (b + 1) * KD)
                for j in range(KD):
                    dve.wait_ge(yb_ps, b * KD + j + 1)
                    nc.vector.tensor_tensor(u[:, j, :], u[:, j, :], yb_bank[j % 4][:, :], ALU.add).then_inc(yu_done, 1)
                    if j in (1, 3) and not last:
                        for t in (j - 1, j):
                            step_size(b + 1, t)
                        inputs(b + 1, j // JQ)

            sequences(dve, sequence)
            for part in range(2):
                times_g(NB - 1, part)
                for c in range(part * TC // 2, (part + 1) * TC // 2):
                    residual(NB - 1, c)

        @block.tensor
        def _(pe):
            pe.wait_ge(const_in, N_CONST)

            def transpose_x(c, k):
                if k == 0:
                    pe.wait_ge(xn_done, (c + 1) * TC)
                for t in range(TC):
                    done = nc.tensor.transpose(xT_bank[k][:, t * P:(t + 1) * P], xt[:, t, k * P:(k + 1) * P], ident[:, :])
                done.then_inc(xT_ps, 1)

            def from_x(bank, k, part, ready):
                hi, lo = w_hi[:, (k - E_GATE) % HI_RING, part], w_lo[:, (k - E_GATE) % HI_RING, part]
                products = [(w, xs, kk) for w, xs in ((lo, x_hi), (hi, x_lo), (hi, x_hi)) for kk in range(KH)]
                for p, (w, xs, kk) in enumerate(products):
                    done = nc.tensor.matmul(bank[:, :], w[:, kk * P:(kk + 1) * P], xs[:, kk, :],
                                            start=(p == 0), stop=(p == len(products) - 1))
                done.then_inc(ready, 1)

            def to_ssm(dst, t, j):
                return nc.tensor.matmul(dst, un[:, j, t * P:(t + 1) * P], wx[:, j, :], start=(j == 0), stop=(j == KD - 1))

            def transpose_dt(c):
                pe.wait_ge(nrm_done, (c + 1) * 2)
                for t in range(TC):
                    done = nc.tensor.matmul(aux[1][0:G + N, t * P:(t + 1) * P], nrm[:, t, 0:G + N], ident[:, :],
                                            start=True, stop=True)
                done.then_inc(dtT_ps, 1)

            def to_delta(c, j):
                if j == 0:
                    pe.wait_ge(dtT_done, c + 1)
                if j >= 4:
                    pe.wait_ge(del_done, c * KD + j - 3)
                nc.tensor.matmul(pj[j % 4][:, :], wdt[:, j * P:(j + 1) * P], dtB[0:G, :],
                                 start=True, stop=True).then_inc(z_ps, 1)

            for k in range(KH):
                transpose_x(0, k)
            pe.wait_ge(xT_done, KH)
            for j in range(KD):
                if j % 2 == 0:
                    pe.wait_ge(lo_done, j // 2 + 1)
                if 4 <= j < 6:
                    pe.wait_ge(tap_done, (j - 3) * (KC - 1))
                from_x(u_bank[j], E_U + j // 2, j % 2, u_ps)
            pe.wait_ge(tap_done, 4 * (KC - 1))
            for j in range(KD):
                pe.wait_ge(u_done, j + 1)
                for t in range(TC):
                    done = to_ssm(ssm_bank0[t][:, 0:F], t, j)
            done.then_inc(ssm_ps, 1)
            transpose_dt(0)
            pe.wait_ge(tap_done, KD * (KC - 1))
            for j in range(KD):
                to_delta(0, j)

            def out_part(b, e, part, end=False):
                j = 2 * e + part
                if part == 0:
                    pe.wait_ge(w_in[e % W_RING], loaded(b, E_OUT + e, end))
                pe.wait_ge(yg_done, (b - 1) * KD + j + 1)
                for c in range(TC):
                    done = nc.tensor.matmul(pj[c][:, :], u[:, j, c * P:(c + 1) * P], ring[:, e % W_RING, part, :],
                                            start=(j == 0), stop=(j == KD - 1))
                if part == 1:
                    done.then_inc(out_used, 1)

            def sequence(b, first, last):
                def weights(k):
                    if k < E_DOWN:
                        pe.wait_ge(lo_done, split(b, k))
                    else:
                        pe.wait_ge(w_in[k % W_RING], loaded(b, k, last))

                def job(i, part):
                    e = i - AT_OUT
                    if 0 <= e < N_OUT and not first:
                        if e == 0 and part == 0:
                            pe.wait_ge(del_done, (b + 1) * KD)
                        out_part(b, e, part)
                    e = i - AT_GATE
                    if 0 <= e < KD // 2:
                        j = 2 * e + part
                        if part == 0:
                            weights(E_GATE + e)
                        if j >= 6:
                            pe.wait_ge(sg_done, b * KD + j - 5)
                        elif j == 2 and first:
                            pe.wait_ge(del_done, KD)
                        elif j == 2:
                            pe.wait_ge(og_done, b * TC)
                        from_x(gate_bank[j], E_GATE + e, part, gt_ps)
                    t = i - AT_FFN
                    if 0 <= t < KI:
                        if part == 0:
                            weights(E_FFN + t)
                        if t < 2:
                            pe.wait_ge(sg_done, b * KD + 3 + 2 * t + part)
                        else:
                            pe.wait_ge(f_done if part else fs_done, b * KI + t - 1)
                        from_x(pj[(2 * t + part) % 4], E_FFN + t, part, fu_ps if part else fg_ps)
                    if i == AT_XT - 1 and part == 1 and not last:
                        pe.wait_ge(sg_done, (b + 1) * KD)
                        for k in range(2):
                            transpose_x(b + 1, k)
                    if i == AT_XT and part == 0 and not last:
                        pe.wait_ge(f_done, (b + 1) * KI - 1)
                        for k in range(2, KH):
                            transpose_x(b + 1, k)
                    e = i - AT_U
                    if 0 <= e < KD // 2 and not last:
                        j = 2 * e + part
                        if part == 0:
                            weights(E_U + e)
                        if j == 0:
                            pe.wait_ge(f_done, (b + 1) * KI)
                            pe.wait_ge(xT_done, (b + 2) * KH)
                        if 4 <= j < 6:
                            pe.wait_ge(tap_done, ((b + 1) * KD + j - 3) * (KC - 1))
                        from_x(u_bank[j], E_U + e, part, u_ps)
                    e = i - AT_DOWN
                    t = 2 * e + part
                    if 0 <= e and t < KI:
                        if part == 0:
                            weights(E_DOWN + e)
                        if t == 0:
                            pe.wait_ge(f_done, (b + 1) * KI)
                            if not last:
                                pe.wait_ge(tap_done, ((b + 1) * KD + 6) * (KC - 1))
                        for c in range(TC):
                            done = nc.tensor.matmul(pj[c][:, :], S[:, t, c * P:(c + 1) * P],
                                                    ring[:, (E_DOWN + e) % W_RING, part, :],
                                                    start=(t == 0), stop=(t == KI - 1))
                        if part == 1 or t == KI - 1:
                            done.then_inc(dn_used, 1)
                    t = 2 * (i - AT_SSM) + part
                    if 0 <= t < TC and not last:
                        if t == 0:
                            pe.wait_ge(u_done, (b + 2) * KD)
                        for j in range(KD):
                            done = to_ssm(aux[0][:, t * F:(t + 1) * F], t, j)
                        if t == TC - 1:
                            done.then_inc(ssm_ps, 1)
                    if i == AT_DTT and part == 0 and not last:
                        transpose_dt(b + 1)

                if not first:
                    pe.wait_ge(yu_done, b * KD)
                for i in range(UNITS):
                    pe.wait_ge(scan_done, b * SU + (i + 1) * QH)
                    for c in range(TC):
                        if i > 0 or c >= 2:
                            pe.wait_ge(y_done, b * UNITS * TC + i * TC + c - 1)
                        for j in range(JH):
                            done = nc.tensor.transpose(hT[c % 2][:, j * P:(j + 1) * P], h[:, i % 2, j, c * P:(c + 1) * P],
                                                       ident[:, :])
                        done.then_inc(hT_ps, 1)
                        if c % 2 == 1:
                            job(i, c // 2)
                def y_back(j):
                    if j >= 4:
                        pe.wait_ge(yu_done, b * KD + j - 3)
                    for c in range(TC):
                        done = nc.tensor.transpose(yb_bank[j % 4][:, c * P:(c + 1) * P], yT[:, c, j * P:(j + 1) * P],
                                                   ident[:, :])
                    done.then_inc(yb_ps, 1)

                if not last:
                    pe.wait_ge(g_done, (b + 1) * TC)
                    for j in range(2):
                        to_delta(b + 1, j)
                pe.wait_ge(y_done, (b + 1) * UNITS * TC)
                for j in range(0, KD, 2):
                    y_back(j)
                    y_back(j + 1)
                    if j + 2 < KD and not last:
                        to_delta(b + 1, j + 2)
                        to_delta(b + 1, j + 3)

            sequences(pe, sequence)
            pe.wait_ge(g_done, NB * TC)
            for e in range(N_OUT):
                for part in range(2):
                    out_part(NB, e, part, end=True)


def kernel(**inputs):
    import concourse.bacc as bacc
    from concourse.bass_utils import run_bass_kernel_spmd

    def get(name):
        return np.asarray(inputs[name])

    def tiles(w):
        return np.ascontiguousarray(w.reshape(-1, P, w.shape[1]).transpose(1, 0, 2))

    def pad(w):
        return np.concatenate([w, np.zeros((KI * P - I, w.shape[1]), w.dtype)])

    def pad(w, rows):
        return np.concatenate([w, np.zeros((rows - w.shape[0], w.shape[1]), w.dtype)])

    def columns(w):
        return w.reshape(KH, P, -1, P).transpose(2, 1, 0, 3).reshape(-1, P, KH * P)

    def entry(w):
        return w.reshape(-1, 2, P, H).transpose(0, 2, 1, 3)

    w_in = get("L0_attn_W_in").T
    gate, up = (columns(pad(get(f"L0_ffn_{n}"), KI * P).T) for n in ("w_gate", "w_up"))
    entries = np.concatenate([
        entry(get("L0_attn_W_out").T.reshape(KD, P, H)),
        entry(columns(w_in[:, D:])),
        np.stack([gate, up], 2),
        entry(columns(w_in[:, :D])),
        entry(pad(get("L0_ffn_w_down").T, -(-KI // 2) * 2 * P).reshape(-1, P, H)),
    ])
    arrays = {
        "x": get("L0_attn_hidden_states"),
        "w_ring": entries,
        "w_x": tiles(get("L0_attn_Wx").T),
        "w_dt": np.concatenate([get("L0_attn_Wdt").T, get("L0_attn_dt_bias")[None]]),
        "conv_w": tiles(get("L0_attn_conv_w")),
        "conv_b": get("L0_attn_conv_b").reshape(KD, P).T,
        "a_par": tiles(get("L0_attn_A")),
        "d_par": get("L0_attn_D_param").reshape(KD, P).T,
        "ln_w": np.concatenate([get("L0_attn_dt_ln_w"), get("L0_attn_b_ln_w"), get("L0_attn_c_ln_w")]),
        "ident": np.eye(P, dtype=np.float32),
    }
    nc = bacc.Bacc("TRN2", target_bir_lowering=False, num_devices=1, dynamic_dma_scratch_size=256)
    args = []
    for name in arrays:
        arrays[name] = np.ascontiguousarray(arrays[name])
        args.append(nc.dram_tensor(name, arrays[name].shape, mybir.dt.float32, kind="ExternalInput").ap())
    out = nc.dram_tensor("out", (NB, T, H), mybir.dt.float32, kind="ExternalOutput").ap()
    build(nc, *args, out)
    r = run_bass_kernel_spmd(nc, [arrays], core_ids=[0])
    return r.results[0]["out"]
```

```python
import numpy as np
import concourse.bass as bass
from concourse import mybir
from concourse.alu_op_type import AluOpType as ALU
from contextlib import ExitStack

NB, T, H, D, N, R, KC, I = 4, 512, 512, 1024, 16, 32, 4, 1376
P = 128
KH, KD, KI, TC = H // P, D // P, -(-I // P), T // P
HF = 2
JH = KD // HF
JQ = 2
QH = JH // JQ
UNITS = N * HF
F = R + 2 * N
LN_EPS, RMS_EPS = 1e-5, 1e-6
W_RING, HI_RING, B_RING, S_RING, LOG_RING = 2, 2, 2, 3, 6
G = R + 1
FN = F + 1

Z_MAX = 88.0

E_OUT, E_GATE, E_FFN, E_U, E_DOWN = 0, KD // 2, KD, KD + KI, KD + KI + KD // 2
N_OUT, N_DOWN = KD // 2, -(-KI // 2)
ENTRIES = E_DOWN + N_DOWN
SPLITS = E_DOWN - E_GATE
AT_OUT, AT_GATE, AT_FFN = 0, KD // 2, KD
AT_XT = AT_FFN + KI
AT_U = AT_XT + 1
AT_DOWN = AT_U + KD // 2
AT_SSM, AT_DTT = AT_DOWN + 3, UNITS - 2
AT_LN = AT_FFN + 2
END_YB = AT_XT
END_DOWN = 2 * AT_U + 1
END_G = (END_DOWN + KI) // 2 + 1
END_OUT = [2 * (END_G + j) + 1 for j in range(JH)]


def down_at(last):
    return END_DOWN if last else 2 * AT_DOWN


SPLIT_AT = {**{AT_GATE + e: E_GATE + e for e in range(KD // 2 + KI)}, **{AT_U + e - (e < HI_RING): E_U + e for e in range(KD // 2)}}
YB_ORDER = [0, 1, 4, 5, 2, 3, 6, 7]
GATED = [1, 3, 5, KD]


def load_order(last):
    used_at = ([(AT_OUT + e, E_OUT + e) for e in range(N_OUT)]
               + [(-(-down_at(last) // 2) + e, E_DOWN + e) for e in range(N_DOWN)])
    return sorted([(i + 0.5, "row", i) for i in range(UNITS - B_RING)]
                  + [(i + 0.9, "entry", k) for i, k in SPLIT_AT.items() if not (last and k >= E_U)]
                  + [(i + 1.6, "entry", k) for i, k in used_at])


def build(nc, x, w_ring, w_x, w_dt, conv_w, conv_b, a_par, d_par, ln_w, ident_d, out):
    fp32 = mybir.dt.float32
    fp32r = mybir.dt.float32r
    ACT = mybir.ActivationFunctionType
    AX = mybir.AxisListType
    ctx = ExitStack()
    with ctx:
        def sb(name, shape, dtype=fp32):
            return ctx.enter_context(nc.sbuf_tensor("sb_" + name, shape, dtype))

        def ps(name):
            return ctx.enter_context(nc.psum_tensor(name, [P, T], fp32))

        def sem(name):
            return ctx.enter_context(nc.semaphore(name))

        wx = sb("wx", [P, KD, F])
        wdt = sb("wdt", [G, D])
        cw = sb("cw", [P, KD, KC])
        cb = sb("cb", [P, KD])
        apar = sb("apar", [P, KD, N])
        dpar = sb("dpar", [P, KD])
        lnw = sb("lnw", [P, F])
        ident = sb("ident", [P, P])
        half = sb("half", [P, 3 * TC])
        ring = sb("ring", [P, W_RING, 2, H])
        w_hi = sb("w_hi", [P, HI_RING, 2, H], fp32r)
        w_lo = sb("w_lo", [P, HI_RING, 2, H], fp32r)
        x_hi = sb("x_hi", [P, KH, T], fp32r)
        x_lo = sb("x_lo", [P, KH, T], fp32r)
        un = sb("un", [P, KD, T])
        u = sb("u", [P, KD, T])
        delta = sb("delta", [P, KD, T])
        v = sb("v", [P, KD, T])
        sgate = sb("sgate", [P, KD, T])
        ssm = sb("ssm", [P, TC, F])
        nrm = sb("nrm", [P, TC, FN])
        cs = sb("cs", [P, TC, N])
        dtB = sb("dtB", [G + N, T])
        bb = sb("bb", [P, B_RING, T])
        dA = sb("dA", [P, S_RING, JQ, T])
        dBu = sb("dBu", [P, S_RING, JQ, T])
        h = sb("h", [P, 2, JH, T])
        yT = sb("yT", [P, TC, D])
        gffn = sb("gffn", [P, TC, H])
        S = sb("S", [P, KI, T])
        stats = sb("stats", [P, TC, 6])
        mv = sb("mv", [P, 3, TC])
        rstd = sb("rstd", [P, 2, TC])
        ms = sb("ms", [P, 3, TC, 3])
        xt = un[:, 0:TC, :]
        xres = S[:, 0:TC, :]
        o = S[:, TC:2 * TC, :]
        log_r = [S[:, TC + r, :] for r in range(LOG_RING)]

        pj = [ps(f"pj{i}") for i in range(4)]
        aux = [ps(f"aux{i}") for i in range(2)]
        hT = [ps(f"hT{i}") for i in range(2)]
        xT_bank = [aux[0], aux[1], pj[2], pj[3]]
        yb_bank = hT + hT + aux + aux
        end_yb_bank = aux + aux + hT + aux
        z_bank = aux + pj[:2] + aux + aux
        u_bank = [pj[j % 4] for j in range(6)] + aux
        gate_bank = aux + pj + aux
        ssm_bank0 = hT + pj[2:]
        b_dram = nc.dram_tensor("b_rows", [N, T], fp32, kind="Internal").ap()

        const_in = sem("const_in")
        init_done = sem("init_done")
        half_done = sem("half_done")
        w_in = [sem(f"w_in{r}") for r in range(W_RING)]
        x_in = sem("x_in")
        ln_stat = sem("ln_stat")
        ln_aggr = sem("ln_aggr")
        ln_var = sem("ln_var")
        ln_rstd = sem("ln_rstd")
        xn_done = sem("xn_done")
        xT_ps = sem("xT_ps")
        xh_done = sem("xh_done")
        xT_done = sem("xT_done")
        hi_done = sem("hi_done")
        lo_done = sem("lo_done")
        u_ps = sem("u_ps")
        tap0_done = sem("tap0_done")
        tap_done = sem("tap_done")
        th_done = sem("th_done")
        th1_done = sem("th1_done")
        u_done = sem("u_done")
        ssm_ps = sem("ssm_ps")
        sq_done = sem("sq_done")
        ms_done = sem("ms_done")
        mse_done = sem("mse_done")
        rms_done = sem("rms_done")
        nm_done = sem("nm_done")
        nrm_done = sem("nrm_done")
        dtT_ps = sem("dtT_ps")
        dtT_done = sem("dtT_done")
        cs_done = sem("cs_done")
        b_out = sem("b_out")
        b_in = [sem(f"b_in{r}") for r in range(B_RING)]
        z_ps = sem("z_ps")
        sp_done = sem("sp_done")
        del_done = sem("del_done")
        v_done = sem("v_done")
        ud_done = sem("ud_done")
        dA_done = sem("dA_done")
        dBu_done = sem("dBu_done")
        scan_done = sem("scan_done")
        hT_ps = sem("hT_ps")
        y_done = sem("y_done")
        gt_ps = sem("gt_ps")
        gtt_done = sem("gtt_done")
        sg_done = sem("sg_done")
        fg_ps = sem("fg_ps")
        fu_ps = sem("fu_ps")
        fth_done = sem("fth_done")
        fs_done = sem("fs_done")
        f_done = sem("f_done")
        dn_used = sem("dn_used")
        gth_done = sem("gth_done")
        g_done = sem("g_done")
        yb_ps = sem("yb_ps")
        yu_done = sem("yu_done")
        yg_done = sem("yg_done")
        out_used = sem("out_used")
        last_ps = sem("last_ps")
        og_done = sem("og_done")
        o_done = sem("o_done")
        xr_in = sem("xr_in")
        out_dma = sem("out_dma")

        consts = [(wx, w_x), (wdt, w_dt), (cw, conv_w), (cb, conv_b), (apar, a_par), (dpar, d_par), (ident, ident_d)]
        N_CONST = 16 * (len(consts) + 1)
        SU = UNITS * QH

        def loaded(b, k, no_u=False):
            a_seq = len(range(k % W_RING, ENTRIES, W_RING))
            u_seq = len([e for e in range(E_U, E_DOWN) if e % W_RING == k % W_RING])
            return 16 * (b * a_seq + k // W_RING + 1 - (u_seq if no_u else 0))

        def split(b, k):
            return KD // 2 + b * SPLITS + k - E_GATE + 1

        def wait_used(eng, b, k, first):
            if k < E_GATE and first or E_GATE <= k < E_DOWN:
                eng.wait_ge(lo_done, split(b, k) if k >= E_GATE else k + 1)
            elif k < E_GATE:
                eng.wait_ge(out_used, (b - 1) * N_OUT + k + 1)
            else:
                eng.wait_ge(dn_used, b * N_DOWN + k - E_DOWN + 1)

        def sequences(eng, body):
            body(0, True, False)
            with eng.Fori(1, NB - 1) as b:
                body(b, False, False)
            body(NB - 1, False, True)

        def rows(dram, b):
            return dram[bass.ds(b, 1), :, :].rearrange("o (c p) h -> p (o c) h", p=P)

        block = ctx.enter_context(nc.Block())

        @block.sync
        def _(sp):
            def load(k, source):
                sp.dma_start(ring[:, k % W_RING], w_ring[source]).then_inc(w_in[k % W_RING], 16)

            def b_rows(c):
                sp.wait_ge(dtT_done, c + 1)
                sp.dma_start(b_dram, dtB[G:G + N, :]).then_inc(b_out, 16)
                sp.wait_ge(b_out, (c + 1) * 16)
                for n in range(B_RING):
                    sp.dma_start(bb[:, n, :], b_dram[n, :].partition_broadcast(P)).then_inc(b_in[n], 16)

            sp.dma_start(xt, rows(x, 0)).then_inc(x_in, 16)
            for dst, src in consts:
                sp.dma_start(dst[:], src).then_inc(const_in, 16)
            sp.dma_start(lnw[:, :], ln_w.partition_broadcast(P)).then_inc(const_in, 16)
            for e in range(KD // 2):
                if e >= W_RING:
                    sp.wait_ge(lo_done, e - W_RING + 1)
                load(e, E_U + e)
            b_rows(0)

            def sequence(b, first, last):
                for _, what, k in load_order(last):
                    if what == "row":
                        m = k + B_RING
                        sp.wait_ge(dBu_done, b * SU + (k + 1) * QH)
                        sp.dma_start(bb[:, m % B_RING, :], b_dram[m % N, :].partition_broadcast(P)).then_inc(b_in[m % B_RING], 16)
                    elif not (first and k + W_RING < E_GATE):
                        nxt = k + W_RING
                        while last and E_U <= nxt < E_DOWN:
                            nxt += W_RING
                        wait_used(sp, b, k, first)
                        load(k % W_RING, nxt if nxt < ENTRIES else E_OUT + k % W_RING)
                sp.dma_start(xres, rows(x, b)).then_inc(xr_in, 16)
                if not last:
                    b_rows(b + 1)

            sequences(sp, sequence)
            for k in range(W_RING, N_OUT):
                wait_used(sp, NB, k - W_RING, False)
                load(k, E_OUT + k)
            for c in range(TC):
                sp.wait_ge(o_done, (NB - 1) * TC + c + 1)
                sp.dma_start(out[NB - 1, c * P:(c + 1) * P, :], o[:, c, :]).then_inc(out_dma, 16)
            sp.wait_ge(out_dma, (NB - 1 + TC) * 16)

        @block.scalar
        def _(act):
            act.wait_ge(const_in, N_CONST)
            act.wait_ge(init_done, 4)
            act.wait_ge(half_done, 2)

            def round_x(c):
                for k in range(KH):
                    act.wait_ge(xT_ps, c * KH + k + 1)
                    nc.scalar.copy(x_hi[:, k, :], xT_bank[k][:, :]).then_inc(xh_done, 1)

            def round_w(slot, k):
                nc.scalar.copy(w_hi[:, (k - E_GATE) % HI_RING], ring[:, slot]).then_inc(hi_done, 1)

            def round_entry(b, k):
                act.wait_ge(w_in[k % W_RING], loaded(b, k))
                before = k - HI_RING
                if before < E_GATE:
                    act.wait_ge(u_ps, (b + 1) * KD)
                elif before < E_FFN:
                    act.wait_ge(gt_ps, b * KD + 2 * (before - E_GATE + 1))
                elif before < E_U:
                    act.wait_ge(fu_ps, b * KI + before - E_FFN + 1)
                else:
                    act.wait_ge(u_ps, (b + 1) * KD + 2 * (before - E_U + 1))
                round_w(k % W_RING, k)

            def round_first(e):
                act.wait_ge(w_in[e % W_RING], 16 * (e // W_RING + 1))
                if e >= HI_RING:
                    act.wait_ge(u_ps, 2 * (e - HI_RING + 1))
                round_w(e % W_RING, E_U + e)

            def first_tap(c, j):
                act.wait_ge(u_ps, c * KD + j + 1)
                nc.scalar.activation(un[:, j, :], u_bank[j][:, :], ACT.Identity, bias=cb[:, j:j + 1],
                                     scale=cw[:, j, KC - 1:KC]).then_inc(tap0_done, 1)

            def conv_tanh(c, j):
                act.wait_ge(tap_done, (c * KD + j + 1) * (KC - 1))
                if j >= TC:
                    act.wait_ge(u_done, c * KD + j - TC + 1)
                nc.scalar.activation(gffn[:, j % TC, :], un[:, j, :], ACT.Tanh).then_inc(th_done, 1)

            def conv_plus1(c, j):
                act.wait_ge(th_done, c * KD + j + 1)
                nc.scalar.activation(gffn[:, j % TC, :], gffn[:, j % TC, :], ACT.Copy, bias=1.0).then_inc(th1_done, 1)

            def squares(c):
                act.wait_ge(ssm_ps, c + 1)
                copy_squares(slice(0, TC), aux[0][:, 0:TC * F].rearrange("p (c f) -> p c f", f=F))

            def copy_squares(t, p_ssm):
                nc.scalar.copy(ssm[:, t, :], p_ssm)
                nc.scalar.activation(nrm[:, t, 0:R], p_ssm[:, :, 0:R], ACT.Square)
                nc.scalar.activation(nrm[:, t, G:FN], p_ssm[:, :, R:F], ACT.Square).then_inc(sq_done, 1)

            def hand_dt(c):
                act.wait_ge(dtT_ps, c + 1)
                if not (isinstance(c, int) and c == 0):
                    act.wait_ge(dBu_done, c * SU)
                nc.scalar.copy(dtB[:, :], aux[1][0:G + N, :]).then_inc(dtT_done, 1)
                nc.scalar.preload_act_table_set("natural_log_exp_and_others")

            def softplus(c, p):
                pair = (2 * p, 2 * p + 1)
                for j in pair:
                    act.wait_ge(z_ps, c * KD + j + 1)
                    if j >= LOG_RING:
                        act.wait_ge(del_done, c * KD + j - LOG_RING + 1)
                    nc.scalar.activation(log_r[j % LOG_RING], z_bank[j][:, :], ACT.Exp).then_inc(sp_done, 1)
                for j in pair:
                    act.wait_ge(sp_done, c * 2 * KD + 4 * p + j % 2 + 1)
                    nc.scalar.activation(log_r[j % LOG_RING], log_r[j % LOG_RING], ACT.Ln, bias=1.0).then_inc(sp_done, 1)

            for e in range(HI_RING):
                round_first(e)
            round_x(0)
            for j in range(KD + 1):
                if j < KD:
                    first_tap(0, j)
                    if j % 2 == 1 and j // 2 + HI_RING < KD // 2:
                        round_first(j // 2 + HI_RING)
                if j > 0:
                    conv_tanh(0, j - 1)
                    conv_plus1(0, j - 1)
            act.wait_ge(ssm_ps, 1)
            for t in range(TC):
                copy_squares(slice(t, t + 1), ssm_bank0[t][:, 0:F].unsqueeze(1))
            hand_dt(0)

            def sequence(b, first, last):
                def decay(i, q):
                    n, hf, s = i % N, i // N, i * QH + q
                    if n == 0:
                        act.wait_ge(del_done, b * KD + hf * JH + (q + 1) * JQ)
                    if s >= S_RING:
                        act.wait_ge(scan_done, b * SU + s - S_RING + 1)
                    for e in range(JQ):
                        j = hf * JH + q * JQ + e
                        done = nc.scalar.activation(dA[:, s % S_RING, e, 1:T], delta[:, j, 1:T], ACT.Exp,
                                                    scale=apar[:, j, n:n + 1])
                    done.then_inc(dA_done, 1)

                def side(i):
                    e = i - AT_GATE - 1
                    if 0 <= e < KD // 2:
                        if e == 0 and not first:
                            act.wait_ge(out_used, b * N_OUT)
                        for j in (2 * e, 2 * e + 1):
                            nc.scalar.activation(u[:, j, :], un[:, j, :], ACT.Copy,
                                                 scale=dpar[:, j:j + 1]).then_inc(ud_done, 1)
                    if i == AT_GATE + 5 and not last:
                        act.wait_ge(ud_done, (b + 1) * KD)
                        act.wait_ge(v_done, (b + 1) * (KD // JQ))
                        act.dma_start(xt, rows(x, b + 1)).then_inc(x_in, 16)
                    if i == AT_FFN + 3 and not first:
                        act.wait_ge(o_done, b * TC)
                        act.dma_start(rows(out, b - 1), o).then_inc(out_dma, 16)
                    e = i - AT_GATE - 2
                    if 0 <= e < KD // 2:
                        for j in (2 * e, 2 * e + 1):
                            act.wait_ge(gt_ps, b * KD + j + 1)
                            nc.scalar.activation(sgate[:, j, :], gate_bank[j][:, :], ACT.Tanh, scale=0.5).then_inc(gtt_done, 1)
                    t = i - AT_FFN - 2
                    if 0 <= t < KI:
                        act.wait_ge(fg_ps, b * KI + t + 1)
                        if t >= TC:
                            act.wait_ge(fs_done, b * KI + t - TC + 1)
                        nc.scalar.activation(gffn[:, t % TC, :], pj[2 * t % 4][:, :], ACT.Tanh, scale=0.5).then_inc(fth_done, 1)
                    e = i - AT_U - 4
                    if 0 <= e < KD // 2 and not last:
                        if e == 0:
                            act.wait_ge(fs_done, (b + 1) * KI)
                        for j in (2 * e, 2 * e + 1):
                            conv_tanh(b + 1, j)
                        for j in (2 * e, 2 * e + 1):
                            conv_plus1(b + 1, j)
                    e = i - AT_U - 2
                    if 0 <= e < KD // 2 and not last:
                        for j in (2 * e, 2 * e + 1):
                            first_tap(b + 1, j)
                    if i == AT_SSM + 3 and not last:
                        squares(b + 1)
                    if i == (END_G if last else UNITS - 1):
                        act.wait_ge(fs_done, (b + 1) * KI)
                        if not last:
                            act.wait_ge(u_done, (b + 2) * KD)
                        act.wait_ge(dn_used, (b + 1) * N_DOWN)
                        for c in range(TC):
                            nc.scalar.activation(gffn[:, c, :], pj[c][:, :], ACT.Tanh, scale=0.5).then_inc(gth_done, 1)

                for i in range(UNITS):
                    for q in range(QH):
                        if i == 0 and q == 0:
                            for p in range(JH // 2):
                                softplus(b, p)
                        decay(i, q)
                        if q == 0:
                            side(i)
                    if i in (2, 4):
                        softplus(b, 1 + i // 2)
                    if i in SPLIT_AT and not (last and SPLIT_AT[i] >= E_U):
                        round_entry(b, SPLIT_AT[i])
                    if i == AT_XT + 1 and not last:
                        round_x(b + 1)
                if not last:
                    hand_dt(b + 1)

            sequences(act, sequence)

        @block.gpsimd
        def _(pool):
            pool.wait_ge(init_done, 4)

            def power_ln(c):
                pool.wait_ge(ln_var, c + 1)
                nc.gpsimd.tensor_tensor(rstd[:, 1, :], rstd[:, 0, :], half[:, 0:TC], ALU.pow).then_inc(ln_rstd, 1)

            def power_rms(c):
                pool.wait_ge(mse_done, (c + 1) * 2)
                nc.gpsimd.tensor_tensor(ms[:, 2].rearrange("p c g -> p (c g)"), ms[:, 1].rearrange("p c g -> p (c g)"),
                                        half[:, :], ALU.pow).then_inc(rms_done, 1)

            def rest_w(slot, k, count):
                pool.wait_ge(hi_done, count)
                nc.gpsimd.tensor_tensor(w_lo[:, (k - E_GATE) % HI_RING], ring[:, slot], w_hi[:, (k - E_GATE) % HI_RING].bitcast(fp32),
                                        ALU.subtract).then_inc(lo_done, 1)

            def times_gate(b, first_j, end_j):
                for j in range(first_j, end_j):
                    pool.wait_ge(yu_done, b * KD + j + 1)
                    nc.gpsimd.tensor_tensor(u[:, j, :], u[:, j, :], sgate[:, j, :], ALU.mult).then_inc(yg_done, 1)

            def conv_silu(c, j):
                pool.wait_ge(th1_done, c * KD + j + 1)
                nc.gpsimd.tensor_tensor(un[:, j, :], gffn[:, j % TC, :], un[:, j, :], ALU.mult).then_inc(u_done, 1)

            power_ln(0)
            for e in range(HI_RING):
                rest_w(e % W_RING, E_U + e, e + 1)
            for j in range(KD):
                e = j // 2 + HI_RING
                if j % 2 == 0 and e < KD // 2:
                    rest_w(e % W_RING, E_U + e, e + 1)
                conv_silu(0, j)
            power_rms(0)

            def sequence(b, first, last):
                for i in range(UNITS):
                    n, hf = i % N, i // N
                    if i == AT_LN + TC + 2 and not last:
                        power_ln(b + 1)
                    pool.wait_ge(b_in[i % B_RING], b * 16 * (UNITS // B_RING) + 16 * (i // B_RING + 1))
                    for q in range(QH):
                        s = i * QH + q
                        j = hf * JH + q * JQ
                        if n == 0:
                            pool.wait_ge(v_done, b * (KD // JQ) + j // JQ + 1)
                        if s >= S_RING:
                            pool.wait_ge(scan_done, b * SU + s - S_RING + 1)
                        nc.gpsimd.tensor_tensor(dBu[:, s % S_RING, :, :], v[:, j:j + JQ, :],
                                                bb[:, i % B_RING, :].unsqueeze(1).to_broadcast([P, JQ, T]),
                                                ALU.mult).then_inc(dBu_done, 1)
                    if i in SPLIT_AT and not (last and SPLIT_AT[i] >= E_U):
                        k = SPLIT_AT[i]
                        rest_w(k % W_RING, k, split(b, k))
                    e = i - AT_U - 4
                    if 0 <= e < KD // 2 and not last:
                        for j in (2 * e, 2 * e + 1):
                            conv_silu(b + 1, j)
                    if i < len(GATED) - 1 and not first:
                        times_gate(b - 1, GATED[i], GATED[i + 1])
                    if last and END_YB + 2 <= i < END_YB + 4:
                        times_gate(b, 2 * (i - END_YB - 2), 2 * (i - END_YB - 1))
                if not last:
                    power_rms(b + 1)
                    times_gate(b, 0, GATED[0])

            sequences(pool, sequence)
            times_gate(NB - 1, JH, KD)

        @block.vector
        def _(dve):
            nc.vector.memset(half[:, :], -0.5).then_inc(init_done, 1)
            nc.vector.memset(nrm[:, :, R:G], 1.0).then_inc(init_done, 1)
            for e in range(JQ):
                nc.vector.memset(dA[:, :, e, 0:1], 0.0).then_inc(init_done, 1)

            def ln_stats(c, t):
                if t == 0:
                    dve.wait_ge(x_in, (c + 1) * 16)
                nc.vector.bn_stats(stats[:, t, :], xt[:, t, :]).then_inc(ln_stat, 1)

            def ln_variance(c):
                dve.wait_ge(ln_stat, (c + 1) * TC)
                nc.vector.tensor_tensor(mv[:, 0, :], stats[:, :, 1], stats[:, :, 4], ALU.add).then_inc(ln_aggr, 1)
                nc.vector.tensor_tensor(mv[:, 1, :], stats[:, :, 1], stats[:, :, 4], ALU.subtract).then_inc(ln_aggr, 1)
                nc.vector.tensor_tensor(mv[:, 2, :], stats[:, :, 2], stats[:, :, 5], ALU.add).then_inc(ln_aggr, 1)
                dve.wait_ge(ln_aggr, c * 6 + 3)
                nc.vector.tensor_scalar(mv[:, 0, :], mv[:, 0, :], 0.5, None, ALU.mult).then_inc(ln_aggr, 1)
                nc.vector.tensor_tensor(mv[:, 1, :], mv[:, 1, :], mv[:, 1, :], ALU.mult).then_inc(ln_aggr, 1)
                nc.vector.tensor_scalar(mv[:, 2, :], mv[:, 2, :], 1.0 / H, LN_EPS, ALU.mult, ALU.add).then_inc(ln_aggr, 1)
                dve.wait_ge(ln_aggr, c * 6 + 6)
                nc.vector.scalar_tensor_tensor(out=rstd[:, 0, :], in0=mv[:, 1, :], scalar=0.25, in1=mv[:, 2, :],
                                               op0=ALU.mult, op1=ALU.add).then_inc(ln_var, 1)

            def ln_apply(c, t):
                if t == 0:
                    dve.wait_ge(ln_rstd, c + 1)
                nc.vector.tensor_scalar(xt[:, t, :], xt[:, t, :], mv[:, 0, t:t + 1], rstd[:, 1, t:t + 1],
                                        ALU.subtract, ALU.mult).then_inc(xn_done, 1)

            def rest_x(c, first_k, end_k):
                for k in range(first_k, end_k):
                    dve.wait_ge(xh_done, c * KH + k + 1)
                    nc.vector.tensor_tensor(x_lo[:, k, :], xT_bank[k][:, :], x_hi[:, k, :].bitcast(fp32),
                                            ALU.subtract).then_inc(xT_done, 1)

            def taps(c, j):
                acc = un[:, j, :]
                for k in range(1, KC):
                    if k == 1:
                        dve.wait_ge(tap0_done, c * KD + j + 1)
                    else:
                        dve.wait_ge(tap_done, (c * KD + j) * (KC - 1) + k - 1)
                    nc.vector.scalar_tensor_tensor(
                        out=acc[:, k:T], in0=u_bank[j][:, 0:T - k], scalar=cw[:, j, KC - 1 - k:KC - k],
                        in1=acc[:, k:T], op0=ALU.mult, op1=ALU.add).then_inc(tap_done, 1)

            def rms_squares(c):
                dve.wait_ge(sq_done, c + TC)
                nc.vector.tensor_reduce(ms[:, 0, :, 0:1], nrm[:, :, 0:R], AX.X, ALU.add).then_inc(ms_done, 1)
                nc.vector.tensor_reduce(ms[:, 0, :, 1:3], nrm[:, :, G:FN].rearrange("p c (g n) -> p c g n", n=N),
                                        AX.X, ALU.add).then_inc(ms_done, 1)
                dve.wait_ge(ms_done, (c + 1) * 2)
                nc.vector.tensor_scalar(ms[:, 1, :, 0:1], ms[:, 0, :, 0:1], 1.0 / R, RMS_EPS, ALU.mult, ALU.add).then_inc(mse_done, 1)
                nc.vector.tensor_scalar(ms[:, 1, :, 1:3], ms[:, 0, :, 1:3], 1.0 / N, RMS_EPS, ALU.mult, ALU.add).then_inc(mse_done, 1)

            def rms_apply(c):
                dve.wait_ge(rms_done, c + 1)
                nc.vector.tensor_tensor(ssm[:, :, 0:R], ssm[:, :, 0:R], ms[:, 2, :, 0:1].to_broadcast([P, TC, R]),
                                        ALU.mult).then_inc(nm_done, 1)
                bc = ssm[:, :, R:F].rearrange("p c (g n) -> p c g n", n=N)
                nc.vector.tensor_tensor(bc, bc, ms[:, 2, :, 1:3].unsqueeze(3).to_broadcast([P, TC, 2, N]),
                                        ALU.mult).then_inc(nm_done, 1)
                dve.wait_ge(nm_done, (c + 1) * 2)
                w = lnw[:, :].unsqueeze(1)
                nc.vector.tensor_tensor(nrm[:, :, 0:R], ssm[:, :, 0:R], w[:, :, 0:R].to_broadcast([P, TC, R]),
                                        ALU.mult).then_inc(nrm_done, 1)
                nc.vector.tensor_tensor(nrm[:, :, G:FN], ssm[:, :, R:F], w[:, :, R:F].to_broadcast([P, TC, 2 * N]),
                                        ALU.mult).then_inc(nrm_done, 1)

            def hand_c(c):
                dve.wait_ge(nrm_done, (c + 1) * 2)
                nc.vector.tensor_copy(cs[:, :, :], nrm[:, :, G + N:FN]).then_inc(cs_done, 1)

            def step_size(c, j):
                dve.wait_ge(sp_done, c * 2 * KD + 4 * (j // 2) + 3 + j % 2)
                nc.vector.scalar_tensor_tensor(out=delta[:, j, :], in0=log_r[j % LOG_RING], scalar=Z_MAX, in1=z_bank[j][:, :],
                                               op0=ALU.min, op1=ALU.max).then_inc(del_done, 1)

            def inputs(c, p):
                j = p * JQ
                dve.wait_ge(del_done, c * KD + j + JQ)
                nc.vector.tensor_tensor(v[:, j:j + JQ, :], delta[:, j:j + JQ, :], un[:, j:j + JQ, :],
                                        ALU.mult).then_inc(v_done, 1)

            def add_ud(b, j, bank, order):
                dve.wait_ge(yb_ps, b * KD + order.index(j) + 1)
                nc.vector.tensor_tensor(u[:, j, :], u[:, j, :], bank[j][:, :], ALU.add).then_inc(yu_done, 1)

            def times_g(b, part):
                if part == 0:
                    dve.wait_ge(out_used, (b + 1) * N_OUT)
                for c in range(part * TC // 2, (part + 1) * TC // 2):
                    scale_g(c)

            def scale_g(c):
                nc.vector.scalar_tensor_tensor(out=o[:, c, :], in0=pj[c][:, :], scalar=0.25, in1=gffn[:, c, :],
                                               op0=ALU.mult, op1=ALU.mult).then_inc(og_done, 1)

            def residual(b, c):
                if c == 0:
                    dve.wait_ge(xr_in, (b + 1) * 16)
                dve.wait_ge(og_done, b * TC + c + 1)
                nc.vector.tensor_tensor(o[:, c, :], o[:, c, :], xres[:, c, :], ALU.add).then_inc(o_done, 1)

            for t in range(TC):
                ln_stats(0, t)
            ln_variance(0)
            dve.wait_ge(const_in, N_CONST)
            nc.vector.tensor_scalar(cw[:, :, :], cw[:, :, :], 0.5, None, ALU.mult).then_inc(half_done, 1)
            nc.vector.tensor_scalar(cb[:, :], cb[:, :], 0.5, None, ALU.mult).then_inc(half_done, 1)
            for t in range(TC):
                ln_apply(0, t)
            rest_x(0, 0, KH)
            dve.wait_ge(half_done, 2)
            for j in range(KD):
                taps(0, j)
            rms_squares(0)
            rms_apply(0)
            hand_c(0)
            for j in range(JH):
                step_size(0, j)
                if j % JQ == JQ - 1:
                    inputs(0, j // JQ)

            def sequence(b, first, last):
                def add_state(i, c):
                    n, hf = i % N, i // N
                    y = yT[:, c, hf * JH * P:(hf + 1) * JH * P]
                    cn = cs[:, c, n:n + 1]
                    dve.wait_ge(hT_ps, b * UNITS * TC + i * TC + c + 1)
                    if n == 0:
                        dve.wait_ge(cs_done, b + 1)
                        nc.vector.tensor_scalar(y, hT[c % 2][:, :], cn, None, ALU.mult).then_inc(y_done, 1)
                    else:
                        dve.wait_ge(y_done, b * UNITS * TC + (i - 1) * TC + c + 1)
                        nc.vector.scalar_tensor_tensor(out=y, in0=hT[c % 2][:, :], scalar=cn, in1=y,
                                                       op0=ALU.mult, op1=ALU.add).then_inc(y_done, 1)

                def ffn_tile(t, part):
                    if part == 0:
                        if t == 0 and not first:
                            dve.wait_ge(o_done, b * TC)
                        if t == TC and not first:
                            dve.wait_ge(out_dma, b * 16)
                        dve.wait_ge(fth_done, b * KI + t + 1)
                        nc.vector.scalar_tensor_tensor(out=S[:, t, :], in0=gffn[:, t % TC, :], scalar=1.0, in1=pj[2 * t % 4][:, :],
                                                       op0=ALU.add, op1=ALU.mult).then_inc(fs_done, 1)
                    else:
                        dve.wait_ge(fu_ps, b * KI + t + 1)
                        dve.wait_ge(fs_done, b * KI + t + 1)
                        nc.vector.scalar_tensor_tensor(out=S[:, t, :], in0=S[:, t, :], scalar=0.5, in1=pj[(2 * t + 1) % 4][:, :],
                                                       op0=ALU.mult, op1=ALU.mult).then_inc(f_done, 1)

                def ffn_silu(c):
                    dve.wait_ge(gth_done, b * TC + c + 1)
                    nc.vector.scalar_tensor_tensor(out=gffn[:, c, :], in0=gffn[:, c, :], scalar=1.0, in1=pj[c][:, :],
                                                   op0=ALU.add, op1=ALU.mult).then_inc(g_done, 1)

                def side(i, part):
                    if i in (2, 4):
                        step_size(b, i + 2 + part)
                    if i in (3, 5) and part == 0:
                        inputs(b, (i + 1) // 2)
                    if i == AT_GATE + 1 and not first:
                        times_g(b - 1, part)
                    if 0 <= i - AT_GATE - 2 < TC and part == 1 and not first:
                        residual(b - 1, i - AT_GATE - 2)
                    e = i - AT_GATE - 2
                    if 0 <= e < KD // 2:
                        j = 2 * e + part
                        dve.wait_ge(gtt_done, b * KD + j + 1)
                        nc.vector.scalar_tensor_tensor(out=sgate[:, j, :], in0=sgate[:, j, :], scalar=1.0,
                                                       in1=gate_bank[j][:, :], op0=ALU.add, op1=ALU.mult).then_inc(sg_done, 1)
                    t = i - AT_FFN - 2
                    if 0 <= t < KI:
                        ffn_tile(t, part)
                    if not last:
                        if 0 <= i - AT_LN < TC and part == 1:
                            ln_stats(b + 1, i - AT_LN)
                        if i == AT_LN + TC and part == 1:
                            ln_variance(b + 1)
                        if 0 <= i - AT_LN - TC - 2 < 2:
                            ln_apply(b + 1, 2 * (i - AT_LN - TC - 2) + part)
                        if i == AT_XT + 1:
                            rest_x(b + 1, 2 * part, 2 * part + 2)
                        e = i - AT_U - 2
                        if 0 <= e < KD // 2:
                            taps(b + 1, 2 * e + part)
                        if i == AT_SSM + 3 and part == 0:
                            rms_squares(b + 1)
                        if i == AT_SSM + 3 and part == 1:
                            rms_apply(b + 1)
                    j = 2 * (i - END_YB - 1) + part
                    if last and 0 <= j < JH:
                        if j == 0:
                            dve.wait_ge(ud_done, (b + 1) * KD)
                        add_ud(b, j, end_yb_bank, range(KD))
                    if last and i == END_G and part == 0:
                        for c in range(TC):
                            ffn_silu(c)
                    if not last and i == UNITS - 1 and part == 1:
                        for c in range(2):
                            ffn_silu(c)

                for i in range(UNITS):
                    for q in range(QH):
                        s = i * QH + q
                        dve.wait_ge(dA_done, b * SU + s + 1)
                        dve.wait_ge(dBu_done, b * SU + s + 1)
                        if i >= 2 and q == 0:
                            dve.wait_ge(hT_ps, b * UNITS * TC + (i - 1) * TC)
                        nc.vector.tensor_tensor_scan(
                            h[:, i % 2, q * JQ:(q + 1) * JQ, :].rearrange("p j t -> p (j t)"),
                            dA[:, s % S_RING].rearrange("p j t -> p (j t)"),
                            dBu[:, s % S_RING].rearrange("p j t -> p (j t)"),
                            0.0, ALU.mult, ALU.add).then_inc(scan_done, 1)
                        if i > 0:
                            for c in range(q * TC // QH, (q + 1) * TC // QH):
                                add_state(i - 1, c)
                        if i == 0 and not first:
                            for j in (1, 2) if q == 0 else (3, 4, 5):
                                add_ud(b - 1, j, yb_bank, YB_ORDER)
                        if i == 1 and q == 0 and not first:
                            for j in (6, 7):
                                add_ud(b - 1, j, yb_bank, YB_ORDER)
                        side(i, q)
                for c in range(TC):
                    add_state(UNITS - 1, c)
                    if c == 1 and not last:
                        for t in range(2, TC):
                            ffn_silu(t)
                if not last:
                    dve.wait_ge(y_done, (b + 1) * UNITS * TC)
                    hand_c(b + 1)
                    dve.wait_ge(ud_done, (b + 1) * KD)
                    for p in range(JH // JQ):
                        for j in range(p * JQ, (p + 1) * JQ):
                            step_size(b + 1, j)
                        if p == 0:
                            add_ud(b, 0, yb_bank, YB_ORDER)
                        inputs(b + 1, p)
                else:
                    for j in range(JH, KD):
                        add_ud(b, j, end_yb_bank, range(KD))

            sequences(dve, sequence)
            for c in range(TC):
                dve.wait_ge(last_ps, c + 1)
                scale_g(c)
                residual(NB - 1, c)

        @block.tensor
        def _(pe):
            pe.wait_ge(const_in, N_CONST)

            def transpose_x(c, k):
                if k == 0:
                    pe.wait_ge(xn_done, (c + 1) * TC)
                for t in range(TC):
                    done = nc.tensor.transpose(xT_bank[k][:, t * P:(t + 1) * P], xt[:, t, k * P:(k + 1) * P], ident[:, :])
                done.then_inc(xT_ps, 1)

            def from_x(bank, k, part, ready, new_x=None):
                hi, lo = w_hi[:, (k - E_GATE) % HI_RING, part], w_lo[:, (k - E_GATE) % HI_RING, part]
                products = [(w, xs, kk) for w, xs in ((lo, x_hi), (hi, x_lo), (hi, x_hi)) for kk in range(KH)]
                for p, (w, xs, kk) in enumerate(products):
                    if new_x is not None and p <= KH:
                        pe.wait_ge(xT_done if p == KH else xh_done, new_x + (KH if p == KH else p + 1))
                    done = nc.tensor.matmul(bank[:, :], w[:, kk * P:(kk + 1) * P], xs[:, kk, :],
                                            start=(p == 0), stop=(p == len(products) - 1))
                done.then_inc(ready, 1)

            def to_ssm(dst, t, j):
                return nc.tensor.matmul(dst, un[:, j, t * P:(t + 1) * P], wx[:, j, :], start=(j == 0), stop=(j == KD - 1))

            def transpose_dt(c):
                pe.wait_ge(nrm_done, (c + 1) * 2)
                for t in range(TC):
                    done = nc.tensor.matmul(aux[1][0:G + N, t * P:(t + 1) * P], nrm[:, t, 0:G + N], ident[:, :],
                                            start=True, stop=True)
                done.then_inc(dtT_ps, 1)

            def to_delta(c, j):
                if j == 0:
                    pe.wait_ge(dtT_done, c + 1)
                if j >= 4:
                    pe.wait_ge(del_done, c * KD + (j - 3 if j < 6 else j - 1))
                nc.tensor.matmul(z_bank[j][:, :], wdt[:, j * P:(j + 1) * P], dtB[0:G, :],
                                 start=True, stop=True).then_inc(z_ps, 1)

            for k in range(KH):
                transpose_x(0, k)
            pe.wait_ge(xT_done, KH)
            for j in range(KD):
                if j % 2 == 0:
                    pe.wait_ge(lo_done, j // 2 + 1)
                if 4 <= j < 6:
                    pe.wait_ge(tap_done, (j - 3) * (KC - 1))
                from_x(u_bank[j], E_U + j // 2, j % 2, u_ps)
            pe.wait_ge(tap_done, 4 * (KC - 1))
            for j in range(KD):
                pe.wait_ge(u_done, j + 1)
                for t in range(TC):
                    done = to_ssm(ssm_bank0[t][:, 0:F], t, j)
            done.then_inc(ssm_ps, 1)
            transpose_dt(0)
            pe.wait_ge(tap_done, KD * (KC - 1))
            for j in range(6):
                to_delta(0, j)

            def out_part(b, e, part, end=False):
                j = 2 * e + part
                if part == 0:
                    pe.wait_ge(w_in[e % W_RING], loaded(b, E_OUT + e, end))
                pe.wait_ge(yg_done, (b - 1) * KD + j + 1)
                for c in (2, 3, 0, 1):
                    if j == 0 and c < 2 and not end:
                        pe.wait_ge(del_done, b * KD + c + 3)
                    done = nc.tensor.matmul(pj[c][:, :], u[:, j, c * P:(c + 1) * P], ring[:, e % W_RING, part, :],
                                            start=(j == 0), stop=(j == KD - 1))
                if part == 1:
                    done.then_inc(out_used, 1)

            def sequence(b, first, last):
                def weights(k):
                    if k < E_DOWN:
                        pe.wait_ge(lo_done, split(b, k))
                    else:
                        pe.wait_ge(w_in[k % W_RING], loaded(b, k, last))

                def y_back(j, bank):
                    for c in range(TC):
                        done = nc.tensor.transpose(bank[:, c * P:(c + 1) * P], yT[:, c, j * P:(j + 1) * P], ident[:, :])
                    done.then_inc(yb_ps, 1)

                def job(i, part):
                    if i == 0 and part == 0 and not first:
                        for j in (6, 7):
                            pe.wait_ge(yu_done, (b - 1) * KD + j - 1)
                            y_back(j, yb_bank[j])
                    j = 2 * (i - AT_OUT) + part + 1
                    if j < KD and not first:
                        out_part(b, j // 2, j % 2)
                    if i == 0 and part == 1 and not first:
                        for j in (4, 5):
                            pe.wait_ge(yu_done, (b - 1) * KD + j + 3)
                            to_delta(b, j)
                    if i == 2:
                        to_delta(b, 6 + part)
                    e = i - AT_GATE
                    if 0 <= e < KD // 2:
                        j = 2 * e + part
                        if part == 0:
                            weights(E_GATE + e)
                        if j < 2:
                            pe.wait_ge(del_done, b * KD + 7 + j)
                        if j >= 6:
                            pe.wait_ge(sg_done, b * KD + j - 5)
                        elif j == 2 and first:
                            pe.wait_ge(del_done, KD)
                        elif j == 2:
                            pe.wait_ge(og_done, b * TC)
                        from_x(gate_bank[j], E_GATE + e, part, gt_ps)
                    t = i - AT_FFN
                    if 0 <= t < KI:
                        if part == 0:
                            weights(E_FFN + t)
                        if t < 2:
                            pe.wait_ge(sg_done, b * KD + 3 + 2 * t + part)
                        else:
                            pe.wait_ge(f_done if part else fs_done, b * KI + t - 1)
                        from_x(pj[(2 * t + part) % 4], E_FFN + t, part, fu_ps if part else fg_ps)
                    if i == AT_XT - 1 and part == 1 and not last:
                        pe.wait_ge(sg_done, (b + 1) * KD)
                        for k in range(2):
                            transpose_x(b + 1, k)
                    if i == AT_XT and part == 0 and not last:
                        pe.wait_ge(f_done, (b + 1) * KI - 1)
                        for k in range(2, KH):
                            transpose_x(b + 1, k)
                    e = i - AT_U
                    if 0 <= e < KD // 2 and not last:
                        j = 2 * e + part
                        if part == 0:
                            weights(E_U + e)
                        if j == 0:
                            pe.wait_ge(f_done, (b + 1) * KI)
                        if 4 <= j < 6:
                            pe.wait_ge(tap_done, ((b + 1) * KD + j - 3) * (KC - 1))
                        from_x(u_bank[j], E_U + e, part, u_ps, (b + 1) * KH if j == 0 else None)
                    j = 2 * (i - END_YB) + part
                    if last and 0 <= j < JH:
                        if j == 0:
                            pe.wait_ge(y_done, (b * UNITS + N) * TC)
                        if j >= 2:
                            pe.wait_ge(yu_done, b * KD + j - 1)
                        y_back(j, end_yb_bank[j])
                    t = 2 * i + part - down_at(last)
                    if 0 <= t < KI:
                        e = t // 2
                        if t % 2 == 0:
                            weights(E_DOWN + e)
                        if t == 0:
                            pe.wait_ge(f_done, (b + 1) * KI)
                            if not last:
                                pe.wait_ge(tap_done, ((b + 1) * KD + 4) * (KC - 1))
                        for c in (2, 3, 0, 1):
                            if t == 0 and c < 2 and not last:
                                pe.wait_ge(tap_done, ((b + 1) * KD + 5 + c) * (KC - 1))
                            done = nc.tensor.matmul(pj[c][:, :], S[:, t, c * P:(c + 1) * P],
                                                    ring[:, (E_DOWN + e) % W_RING, t % 2, :],
                                                    start=(t == 0), stop=(t == KI - 1))
                        if t % 2 == 1 or t == KI - 1:
                            done.then_inc(dn_used, 1)
                    if last and 2 * i + part in END_OUT:
                        j = END_OUT.index(2 * i + part)
                        if j == 0:
                            pe.wait_ge(g_done, (b + 1) * TC)
                        out_part(b + 1, j // 2, j % 2, end=True)
                    t = 2 * (i - AT_SSM) + part
                    if 0 <= t < TC and not last:
                        if t == 0:
                            pe.wait_ge(u_done, (b + 2) * KD)
                        for j in range(KD):
                            done = to_ssm(aux[0][:, t * F:(t + 1) * F], t, j)
                        if t == TC - 1:
                            done.then_inc(ssm_ps, 1)
                    if i == AT_DTT and part == 1 and not last:
                        transpose_dt(b + 1)
                    if i == UNITS - 1 and not last:
                        if part == 1:
                            pe.wait_ge(g_done, b * TC + 2)
                        to_delta(b + 1, 2 * part)
                        to_delta(b + 1, 2 * part + 1)

                if not first:
                    pe.wait_ge(yu_done, (b - 1) * KD + JH)
                for i in range(UNITS):
                    pe.wait_ge(scan_done, b * SU + (i + 1) * QH)
                    for c in range(TC):
                        if i > 0 or c >= 2:
                            pe.wait_ge(y_done, b * UNITS * TC + i * TC + c - 1)
                        for j in range(JH):
                            done = nc.tensor.transpose(hT[c % 2][:, j * P:(j + 1) * P], h[:, i % 2, j, c * P:(c + 1) * P],
                                                       ident[:, :])
                        done.then_inc(hT_ps, 1)
                        if c % 2 == 1:
                            job(i, c // 2)
                if not last:
                    pe.wait_ge(y_done, (b + 1) * UNITS * TC)
                    for j in YB_ORDER[:5]:
                        if j >= 4:
                            pe.wait_ge(del_done, (b + 1) * KD + j - 3)
                        if j == 2:
                            pe.wait_ge(yu_done, b * KD + 1)
                        y_back(j, yb_bank[j])
                    pe.wait_ge(g_done, (b + 1) * TC)
                    out_part(b + 1, 0, 0)
                    pe.wait_ge(yu_done, b * KD + 2)
                    y_back(3, yb_bank[3])
                else:
                    pe.wait_ge(y_done, (b + 1) * UNITS * TC)
                    for j in range(JH, KD):
                        y_back(j, end_yb_bank[j])

            sequences(pe, sequence)
            for j in range(len(END_OUT), KD - 2):
                out_part(NB, j // 2, j % 2, end=True)
            e = N_OUT - 1
            pe.wait_ge(w_in[e % W_RING], loaded(NB, E_OUT + e, True))
            pe.wait_ge(yg_done, NB * KD)
            for c in range(TC):
                for part in range(2):
                    done = nc.tensor.matmul(pj[c][:, :], u[:, 2 * e + part, c * P:(c + 1) * P], ring[:, e % W_RING, part, :],
                                            start=False, stop=(part == 1))
                done.then_inc(last_ps, 1)


def kernel(**inputs):
    import concourse.bacc as bacc
    from concourse.bass_utils import run_bass_kernel_spmd

    def get(name):
        return np.asarray(inputs[name])

    def tiles(w):
        return np.ascontiguousarray(w.reshape(-1, P, w.shape[1]).transpose(1, 0, 2))

    def pad(w, rows):
        return np.concatenate([w, np.zeros((rows - w.shape[0], w.shape[1]), w.dtype)])

    def columns(w):
        return w.reshape(KH, P, -1, P).transpose(2, 1, 0, 3).reshape(-1, P, KH * P)

    def entry(w):
        return w.reshape(-1, 2, P, H).transpose(0, 2, 1, 3)

    w_in = get("L0_attn_W_in").T
    gate, up = (columns(pad(get(f"L0_ffn_{n}"), KI * P).T) for n in ("w_gate", "w_up"))
    entries = np.concatenate([
        entry(get("L0_attn_W_out").T.reshape(KD, P, H)),
        entry(columns(w_in[:, D:])),
        np.stack([gate, up], 2),
        entry(columns(w_in[:, :D])),
        entry(pad(get("L0_ffn_w_down").T, -(-KI // 2) * 2 * P).reshape(-1, P, H)),
    ])
    arrays = {
        "x": get("L0_attn_hidden_states"),
        "w_ring": entries,
        "w_x": tiles(get("L0_attn_Wx").T),
        "w_dt": np.concatenate([get("L0_attn_Wdt").T, get("L0_attn_dt_bias")[None]]),
        "conv_w": tiles(get("L0_attn_conv_w")),
        "conv_b": get("L0_attn_conv_b").reshape(KD, P).T,
        "a_par": tiles(get("L0_attn_A")),
        "d_par": get("L0_attn_D_param").reshape(KD, P).T,
        "ln_w": np.concatenate([get("L0_attn_dt_ln_w"), get("L0_attn_b_ln_w"), get("L0_attn_c_ln_w")]),
        "ident": np.eye(P, dtype=np.float32),
    }
    nc = bacc.Bacc("TRN2", target_bir_lowering=False, num_devices=1, dynamic_dma_scratch_size=256)
    args = []
    for name in arrays:
        arrays[name] = np.ascontiguousarray(arrays[name])
        args.append(nc.dram_tensor(name, arrays[name].shape, mybir.dt.float32, kind="ExternalInput").ap())
    out = nc.dram_tensor("out", (NB, T, H), mybir.dt.float32, kind="ExternalOutput").ap()
    build(nc, *args, out)
    r = run_bass_kernel_spmd(nc, [arrays], core_ids=[0])
    return r.results[0]["out"]
```
